# Optimizing a Trainium2 kernel written in Bass

```python
import numpy as np
import jax
import jax.numpy as jnp

def _softmax(x, axis=-1):
    return jax.nn.softmax(x, axis=axis)

def _gelu(x):
    return jax.nn.gelu(x, approximate=True)

def _silu(x):
    return jax.nn.silu(x)

def _sigmoid(x):
    return jax.nn.sigmoid(x)

def _layernorm(x, axis=-1, eps=1e-05):
    m = jnp.mean(x, axis=axis, keepdims=True)
    v = jnp.var(x, axis=axis, keepdims=True)
    return (x - m) / jnp.sqrt(v + eps)

def _scatter_add(tgt, idx, src, axis=0):
    return tgt.at[idx].add(src)

def _segment_sum(src, seg, n):
    return jax.ops.segment_sum(src, seg, n)
kernel_name = 'mk_xattn_seq_d1_seqx_r4_1eb0af'

def setup_inputs(seed: int=0):
    np.random.seed(seed)
    _w = jnp.asarray

    def _rec_inputs():
        import jax
        import jax.numpy as jnp
        _rk = jax.random.key(seed)
        x = -0.0001548 + 1 * jax.random.normal(jax.random.fold_in(_rk, 1), (16, 128, 320), jnp.float32)
        _lenS = 128 - jax.random.randint(jax.random.fold_in(_rk, 7), (16,), 0, max(1, 128 // 4) + 1, jnp.int32)
        _lenS2 = 128 - jax.random.randint(jax.random.fold_in(_rk, 8), (16,), 0, max(1, 128 // 4) + 1, jnp.int32)
        _ctx_768P = jax.random.normal(jax.random.fold_in(_rk, 11), (16, 16, 192), jnp.float32)
        _ctx_768c = jax.random.dirichlet(jax.random.fold_in(_rk, 511), 0.3 * jnp.ones((16,), jnp.float32), (16, 128))
        _ctx_768t = jnp.einsum('bsk,bkd->bsd', _ctx_768c, _ctx_768P)
        _ctx_768t = _ctx_768t * jax.lax.rsqrt(jnp.mean(jnp.square(_ctx_768t)) + 1e-12) * 0.953939
        ctx_768 = 0.00141353 + 0.998943 * (_ctx_768t + 0.3 * jax.random.normal(jax.random.fold_in(_rk, 611), (16, 128, 192), jnp.float32))
        return (x, ctx_768)
    x, ctx_768 = _rec_inputs()

    def _L0_xattn_setup():
        import jax, jax.numpy as jnp
        import numpy as np
        HEADS = 8
        NUM_TOKENS = 4
        CROSS_ATTENTION_DIM = 192

        def _mha(q, k, v, heads=HEADS):
            B, Sq, H = q.shape
            Sk = k.shape[1]
            d = H // heads
            qh = q.reshape(B, Sq, heads, d).transpose(0, 2, 1, 3)
            kh = k.reshape(B, Sk, heads, d).transpose(0, 2, 1, 3)
            vh = v.reshape(B, Sk, heads, d).transpose(0, 2, 1, 3)
            scores = jnp.einsum('bhqd,bhkd->bhqk', qh, kh) * jnp.asarray(d, q.dtype) ** (-0.5)
            probs = jax.nn.softmax(scores, axis=-1)
            out = jnp.einsum('bhqk,bhkd->bhqd', probs, vh)
            return out.transpose(0, 2, 1, 3).reshape(B, Sq, H)
        key = jax.random.key(seed)
        ks = jax.random.split(key, 10)
        B, S, H, CAD, T = (4, 256, 320, CROSS_ATTENTION_DIM, NUM_TOKENS)
        sc = 0.02
        return {'hidden_states': jax.random.normal(ks[0], (B, S, H), jnp.float32), 'encoder_hidden_states': jax.random.normal(ks[1], (B, 77 + T, CAD), jnp.float32), 'Wq': jax.random.normal(ks[2], (H, H), jnp.float32) * sc, 'Wk': jax.random.normal(ks[3], (CAD, H), jnp.float32) * sc, 'Wv': jax.random.normal(ks[4], (CAD, H), jnp.float32) * sc, 'Wq_ca': jax.random.normal(ks[5], (T, H), jnp.float32) * sc, 'Wk_ca': jax.random.normal(ks[6], (CAD, H), jnp.float32) * sc, 'Wv_ca': jax.random.normal(ks[7], (CAD, H), jnp.float32) * sc, 'Wout': jax.random.normal(ks[8], (H, H), jnp.float32) * sc, 'b_out': jnp.zeros((H,), jnp.float32)}
    _L0_xattn_all = _L0_xattn_setup()
    _L0_xattn_in = {k: v for k, v in _L0_xattn_all.items() if k in ('Wq', 'Wk', 'Wv', 'Wq_ca', 'Wk_ca', 'Wv_ca', 'Wout', 'b_out')}
    del _L0_xattn_all
    return {'x': x, 'ctx_768': ctx_768, 'L0_xattn_Wq': _L0_xattn_in['Wq'], 'L0_xattn_Wk': _L0_xattn_in['Wk'], 'L0_xattn_Wv': _L0_xattn_in['Wv'], 'L0_xattn_Wq_ca': _L0_xattn_in['Wq_ca'], 'L0_xattn_Wk_ca': _L0_xattn_in['Wk_ca'], 'L0_xattn_Wv_ca': _L0_xattn_in['Wv_ca'], 'L0_xattn_Wout': _L0_xattn_in['Wout'], 'L0_xattn_b_out': _L0_xattn_in['b_out']}

def reference(x, ctx_768, L0_xattn_Wq, L0_xattn_Wk, L0_xattn_Wv, L0_xattn_Wq_ca, L0_xattn_Wk_ca, L0_xattn_Wv_ca, L0_xattn_Wout, L0_xattn_b_out):
    import jax
    import jax.numpy as jnp

    def _L0_xattn_ref(hidden_states, encoder_hidden_states, Wq, Wk, Wv, Wq_ca, Wk_ca, Wv_ca, Wout, b_out):
        import jax, jax.numpy as jnp
        import numpy as np
        HEADS = 8
        NUM_TOKENS = 4
        CROSS_ATTENTION_DIM = 192

        def _mha(q, k, v, heads=HEADS):
            B, Sq, H = q.shape
            Sk = k.shape[1]
            d = H // heads
            qh = q.reshape(B, Sq, heads, d).transpose(0, 2, 1, 3)
            kh = k.reshape(B, Sk, heads, d).transpose(0, 2, 1, 3)
            vh = v.reshape(B, Sk, heads, d).transpose(0, 2, 1, 3)
            scores = jnp.einsum('bhqd,bhkd->bhqk', qh, kh) * jnp.asarray(d, q.dtype) ** (-0.5)
            probs = jax.nn.softmax(scores, axis=-1)
            out = jnp.einsum('bhqk,bhkd->bhqd', probs, vh)
            return out.transpose(0, 2, 1, 3).reshape(B, Sq, H)
        residual = hidden_states
        unet_size = residual.shape[1]
        end_pos = encoder_hidden_states.shape[1] - NUM_TOKENS
        enc = encoder_hidden_states[:, :end_pos, :]
        ca = encoder_hidden_states[:, end_pos:, :]
        query = hidden_states @ Wq
        keyt = enc @ Wk
        valt = enc @ Wv
        hs = _mha(query, keyt, valt)
        ca_q1 = jnp.einsum('btc,th->bch', ca, Wq_ca)
        indices = np.linspace(0, CROSS_ATTENTION_DIM - 1, unet_size).astype(np.int64)
        ca_q1 = ca_q1[:, indices, :]
        ca_hs1 = _mha(ca_q1, residual, residual)
        ca_q2 = ca_hs1 @ Wq
        ca_k2 = ca @ Wk_ca
        ca_v2 = ca @ Wv_ca
        ca_hs2 = _mha(ca_q2, ca_k2, ca_v2)
        out = hs + ca_hs2
        out = out @ Wout + b_out
        out = out + residual
        return out
    x = _L0_xattn_ref(x, ctx_768, L0_xattn_Wq, L0_xattn_Wk, L0_xattn_Wv, L0_xattn_Wq_ca, L0_xattn_Wk_ca, L0_xattn_Wv_ca, L0_xattn_Wout, L0_xattn_b_out)
    return x

_drawn_inputs = setup_inputs


def setup_inputs(seed=0):
    import zlib

    import numpy as np

    out = dict(_drawn_inputs(seed))
    spreads = {'L0_xattn_b_out': (0.0, 0.1)}
    factors = {'L0_xattn_Wq': 8.0, 'L0_xattn_Wk': 8.0, 'L0_xattn_Wq_ca': 35.944, 'L0_xattn_Wk_ca': 8.0}
    for name, (base, spread) in spreads.items():
        noise = np.random.default_rng([zlib.crc32(name.encode()), seed]).standard_normal(out[name].shape)
        drawn = base * np.exp(spread * noise) if base else spread * noise
        out[name] = jnp.asarray(drawn.astype(out[name].dtype))
    for name, factor in factors.items():
        out[name] = (out[name] * factor).astype(out[name].dtype)
    return out
```

```python
from contextlib import ExitStack

import concourse.bass as bass
from concourse import mybir

F32 = mybir.dt.float32
BF16 = mybir.dt.bfloat16
U32 = mybir.dt.uint32
ACT = mybir.ActivationFunctionType
ALU = mybir.AluOpType
AX = mybir.AxisListType

B, S, HID = 16, 128, 320
CAD, T = 192, 4
HEADS = 8
D = HID // HEADS
SCALE = float(D) ** -0.5
KEYS = S - T
PAIRS = B // 2
KC = 3 * D
NC = 3
PAD = KC * NC
CC = CAD // 2
HT = HEADS * T
Q_COLS = [0, KC, HID - KC]
HEAD_AT = [(0, 0), (0, 1), (0, 2), (1, 0), (1, 1), (1, 2), (2, 1), (2, 2)]
M_PART = [0, 0, 0, 1, 1, 2]
CA_PART = [0, 1, 2, 0, 1, 0]


class At:

    def __init__(self, j, a, b, kind):
        self.j, self.a, self.b, self.kind = j, a, b, kind
        self.par = b % 2

    def lin(self, per, off=0):
        if self.a == 0:
            return per * self.b + off
        return self.j * (per * self.a) + (per * self.b + off)

    def half(self, per, off=0):
        if self.a == 0:
            return per * (self.b // 2) + off
        return self.j * per + (per * (self.b // 2) + off)

    def next(self):
        return At(self.j, self.a, self.b + 1, "next")


class Ring:

    def __init__(self, prologue, first, mid, last, epilogue):
        self.lists = dict(prologue=prologue, first=first, mid=mid, last=last, epilogue=epilogue)

    def no(self, at, name):
        n = {k: len(v) for k, v in self.lists.items()}
        if at == "prologue":
            k = self.lists["prologue"].index(name)
            return k, k % 2
        if at == "epilogue":
            k = n["prologue"] + n["first"] + (PAIRS - 2) * n["mid"] + n["last"]
            k += self.lists["epilogue"].index(name)
            return k, k % 2
        k = self.lists[at.kind].index(name)
        if at.kind == "first":
            k += n["prologue"]
            return k, k % 2
        k += n["prologue"] + n["first"] - n["mid"]
        return at.lin(n["mid"], k), (n["mid"] * at.b + k) % 2


SETUP_A = ["caQ", "WcaT", "WqT0", "WqT2", "k2T", "G1", "VW0", "VW2", "CA1"]
SETUP_D = ["caT", "WqT1", "v2T", "G0", "G2", "VW1", "VW3", "CA0"]
RING_A = Ring(
    SETUP_A + ["xT01", "xT2", "MT", "QT01", "V0", "QT2", "V1"],
    ["xT01", "xT2", "MT", "hs1T0", "hs1T1", "QT01", "V0", "QT2", "V1", "P3T", "hsT0"],
    ["hsT1", "xT01", "xT2", "MT", "hs1T0", "hs1T1", "QT01", "V0", "QT2", "V1", "P3T", "hsT0"],
    ["hsT1", "hs1T0", "hs1T1", "P3T", "hsT0"],
    ["hsT1"],
)
RING_D = Ring(
    SETUP_D + ["ctxT", "KT01", "KT2", "MsT"],
    ["ctxT", "PV0", "KT01", "KT2", "PV1", "sc3", "PV2", "MsT", "PV3", "out0"],
    ["ctxT", "out1", "PV0", "KT01", "KT2", "PV1", "sc3", "PV2", "MsT", "PV3", "out0"],
    ["out1", "PV0", "PV1", "sc3", "PV2", "PV3", "out0"],
    ["out1"],
)


def attention(nc, x, ctx, Wq, Wk, Wv, Wq_ca, Wk_ca, Wv_ca, Wout, b_out, out):
    with ExitStack() as stack:
        def sb(name, shape, dt=F32):
            return stack.enter_context(nc.sbuf_tensor(name, shape, dt))

        def ps(name, dt=F32):
            return stack.enter_context(nc.psum_tensor(name, [128, 512], dt))

        def sem(name):
            return stack.enter_context(nc.semaphore(name))

        wq = sb("wq", [KC, NC, PAD])
        wk = sb("wk", [CC, 2, HID])
        wv = sb("wv", [CC, 2, HID])
        wk_ca = sb("wk_ca", [CC, 2, PAD])
        wv_ca = sb("wv_ca", [CC, 2, PAD])
        wout = sb("wout", [KC, NC, HID])
        wq_ca = sb("wq_ca", [T, PAD])
        bias = sb("bias", [128, HID])
        ident = sb("ident", [128, 128])
        ident16 = sb("ident16", [128, 128], BF16)
        zeros = sb("zeros", [128, B * T])
        hmask = sb("hmask", [KC, NC, HEADS, T])
        ca_all = sb("ca_all", [B * T, CAD])
        ca_sel = sb("ca_sel", [B * T, S])
        caT = sb("caT", [CC, 2, B * T])
        caQ = sb("caQ", [S, B * T])
        ca_rest = sb("ca_rest", [S, B * T])
        ca_parts = sb("ca_parts", [S, 2, B * T], BF16)
        ca_stack = sb("ca_stack", [S, B, 4, 32], BF16)
        ca_rows = sb("ca_rows", [128, B, 4, S], BF16)
        wca_t = sb("wca_t", [KC, NC, T])
        wca_blocks = sb("wca_blocks", [KC, NC, HT])
        wqT = sb("wqT", [KC, NC, PAD])
        k2_blocks = sb("k2_blocks", [KC, NC, B, 3 * T])
        v2_blocks = sb("v2_blocks", [KC, NC, B, HT])
        g = sb("g", [KC, NC, B, HT])
        vw = sb("vw", [128, B // 4, HID])
        x_sb = sb("x_sb", [S, 2, 2, PAD])
        ctx_sb = sb("ctx_sb", [S, 2, 2, CAD])
        xb = sb("xb", [S, 2, 2, HID])
        xT = sb("xT", [KC, NC, 2 * S])
        ctxT = sb("ctxT", [CC, 2, 2 * S])
        qT = sb("qT", [KC, NC, 2 * S])
        k_blocks = sb("k_blocks", [KC, 2, NC, 3, 2, KEYS])
        v_sb = sb("v_sb", [S, 2, 2, HID])
        m = sb("m", [S, 2 * HT])
        m_rest = sb("m_rest", [S, 2 * HT])
        m_parts = sb("m_parts", [S, 2, 2 * HT], BF16)
        m_stack = sb("m_stack", [S, 2, HEADS, 32], BF16)
        m_rows = sb("m_rows", [128, 2, 2, S], BF16)
        neg_max = sb("neg_max", [S, HEADS])
        probs = sb("probs", [S, HEADS, S])
        sums = sb("sums", [S, 2, HEADS])
        recip = sb("recip", [S, 2, HEADS])
        probsT = sb("probsT", [S, HEADS, S])
        hs = sb("hs", [S, 4, PAD])
        hs1T = sb("hs1T", [KC, 2, NC, S])
        hsT = sb("hsT", [KC, 2, NC, S])
        max3 = sb("max3", [S, 2 * HEADS])
        less3 = sb("less3", [S, 2 * HEADS, T])
        exp3 = sb("exp3", [S, 2 * HEADS, T])
        sum3 = sb("sum3", [S, 2, 2 * HEADS])
        probs3 = sb("probs3", [S, 2, 2, 4, HT])
        probs3T = sb("probs3T", [128, 2, S])
        out_sb = sb("out_sb", [S, 2, HID])

        scores = [ps("scores0"), ps("scores1")]
        turned = [ps("turned0"), ps("turned1")]
        bank_a = [ps("bank_a0"), ps("bank_a1")]
        bank_d = [ps("bank_d0"), ps("bank_d1")]

        loaded_wqca = sem("loaded_wqca")
        loaded_ca = sem("loaded_ca")
        loaded_wq = sem("loaded_wq")
        loaded_wca = sem("loaded_wca")
        loaded_wout = sem("loaded_wout")
        loaded_wkv = sem("loaded_wkv")
        loaded_bias = sem("loaded_bias")
        loaded_x = [sem("loaded_x0"), sem("loaded_x1")]
        loaded_ctx = [sem("loaded_ctx0"), sem("loaded_ctx1")]
        stored = [sem("stored0"), sem("stored1")]
        zeroed = sem("zeroed")
        made = sem("made")
        ca_split = sem("ca_split")
        m_step = sem("m_step")
        xb_made = sem("xb_made")
        ca_picked = sem("ca_picked")
        wca_copied = sem("wca_copied")
        a_filled = sem("a_filled")
        a_drained = sem("a_drained")
        d_filled = sem("d_filled")
        d_drained = sem("d_drained")
        scored = sem("scored")
        maxed = sem("maxed")
        exped = sem("exped")
        turned_full = sem("turned_full")
        turned_out = sem("turned_out")
        inverted = sem("inverted")
        max3_made = sem("max3_made")
        exp3_made = sem("exp3_made")
        sum3_made = sem("sum3_made")
        inv3_made = sem("inv3_made")
        probs3_made = sem("probs3_made")

        def g_out(engine, scaled, src, r):
            for c in range(NC):
                heads = 3 if c < 2 else 2
                last = scaled(g[:, r, :, 3 * T * c:3 * T * c + heads * T],
                              src[0:KC, c * B * 3 * T:c * B * 3 * T + B * heads * T]
                                  .rearrange("p (b n) -> p b n", b=B), SCALE)
            return last

        def ca_rows_out(copy, src, n):
            for j in range(4):
                last = copy(ca_rows[32 * j:32 * j + 32, 8 * n:8 * n + 8, j, :],
                            src[32 * j:32 * j + 32, :].bitcast(BF16)
                                .rearrange("p (b q) -> p b q", b=8))
            return last

        block = stack.enter_context(nc.Block())

        def pairs(engine, body):
            body(At(0, 0, 0, "first"))
            with engine.Fori(0, (PAIRS - 2) // 2) as j:
                body(At(j, 2, 1, "mid"))
                body(At(j, 2, 2, "mid"))
            body(At(0, 0, PAIRS - 1, "last"))

        def unit(at, k):
            return at.lin(4, k)

        @block.sync
        def _(sp):
            def load_pair(row, par):
                sp.dma_start(x_sb[:, par, :, 0:HID], x[bass.ds(row, 2)].rearrange("b s h -> s b h")) \
                    .then_inc(loaded_x[par], 16)
                sp.dma_start(ctx_sb[:, par, :, :], ctx[bass.ds(row, 2)].rearrange("b s h -> s b h")) \
                    .then_inc(loaded_ctx[par], 16)

            def store(b, row):
                sp.dma_start(out[bass.ds(row, 1)].rearrange("b s h -> (b s) h"), out_sb[:, b, :]) \
                    .then_inc(stored[b], 16)

            sp.dma_start(ca_all[:, 0:CAD], ctx[:, KEYS:S, :]).then_inc(loaded_ca, 16)
            sp.dma_start(wq_ca[:, 0:HID], Wq_ca).then_inc(loaded_wqca, 16)
            sp.wait_ge(zeroed, 3)
            for w, w_sb, n in ((Wq, wq, loaded_wq), (Wout, wout, loaded_wout)):
                sp.dma_start(w_sb[:, 0:2, 0:HID], w[0:2 * KC, :].rearrange("(c p) n -> p c n", p=KC)) \
                    .then_inc(n, 16)
                sp.dma_start(w_sb[0:HID - 2 * KC, 2, 0:HID], w[2 * KC:HID, :]).then_inc(n, 16)
                if w is Wq:
                    for w2, w2_sb in ((Wk_ca, wk_ca), (Wv_ca, wv_ca)):
                        sp.dma_start(w2_sb[:, :, 0:HID], w2.rearrange("(c p) n -> p c n", p=CC)) \
                            .then_inc(loaded_wca, 16)
            load_pair(0, 0)
            for w2, w2_sb in ((Wk, wk), (Wv, wv)):
                sp.dma_start(w2_sb[:, :, :], w2.rearrange("(c p) n -> p c n", p=CC)) \
                    .then_inc(loaded_wkv, 16)
            sp.dma_start(bias[:, :], b_out.partition_broadcast(128)).then_inc(loaded_bias, 16)
            load_pair(2, 1)

            def fixed(value):
                return value if isinstance(value, int) else sp.snap(value)

            def body(at):
                loads = at.kind != "last" and not (at.a == 0 and at.b + 2 >= PAIRS)
                before, first = fixed(at.lin(2, -1)), fixed(at.lin(2))
                out0_made = fixed(RING_D.no(at, "out0")[0] + 1)
                if at.kind != "first":
                    out1_made = fixed(RING_D.no(at, "out1")[0] + 1)
                if loads:
                    ahead = fixed(at.lin(2, 4))
                    x_used = fixed(RING_D.no(at, "PV1")[0] + 1)
                if at.kind != "first":
                    sp.wait_ge(d_drained, out1_made)
                    store(1, before)
                if loads:
                    sp.wait_ge(d_filled, x_used)
                    load_pair(ahead, at.par)
                sp.wait_ge(d_drained, out0_made)
                store(0, first)

            body(At(0, 0, 0, "first"))
            with sp.Fori(0, (PAIRS - 2) // 2 - 1) as j:
                body(At(j, 2, 1, "mid"))
                body(At(j, 2, 2, "mid"))
            body(At(0, 0, PAIRS - 3, "mid"))
            body(At(0, 0, PAIRS - 2, "mid"))
            body(At(0, 0, PAIRS - 1, "last"))
            sp.wait_ge(d_drained, RING_D.no("epilogue", "out1")[0] + 1)
            store(1, B - 1)
            for b in range(2):
                sp.wait_ge(stored[b], 16 * PAIRS)

        @block.gpsimd
        def _(pool):
            gp = nc.gpsimd
            gp.memset(wq_ca[:, HID:PAD], 0.0).then_inc(zeroed, 1)
            gp.memset(wq[:, 2, :], 0.0).then_inc(zeroed, 1)
            gp.memset(wout[:, 2, :], 0.0).then_inc(zeroed, 1)
            gp.memset(wq[:, 0:2, HID:PAD], 0.0).then_inc(zeroed, 1)
            gp.memset(wk_ca[:, :, HID:PAD], 0.0).then_inc(zeroed, 1)
            gp.memset(wv_ca[:, :, HID:PAD], 0.0).then_inc(zeroed, 1)
            gp.memset(ident[:], 0.0).then_inc(made, 1)
            pool.wait_ge(made, 1)
            gp.affine_select(out=ident[:], in_=ident[:], compare_op=ALU.not_equal, fill=1.0, base=0,
                             pattern=[[-1, 128]], channel_multiplier=1).then_inc(made, 1)
            pool.wait_ge(made, 2)
            gp.tensor_copy(ident16[:], ident[:]).then_inc(made, 1)
            gp.memset(hmask[:], 1.0).then_inc(made, 1)
            pool.wait_ge(made, 4)
            gp.affine_select(out=hmask[:], in_=hmask[:], compare_op=ALU.is_ge, fill=0.0, base=0,
                             pattern=[[KC, NC], [-D, HEADS], [0, T]], channel_multiplier=1) \
                .then_inc(made, 1)
            pool.wait_ge(made, 5)
            gp.affine_select(out=hmask[:], in_=hmask[:], compare_op=ALU.is_ge, fill=0.0, base=D - 1,
                             pattern=[[-KC, NC], [D, HEADS], [0, T]], channel_multiplier=-1) \
                .then_inc(made, 1)
            for t in (x_sb[:, :, :, HID:PAD], hs[:, :, HID:PAD]):
                gp.memset(t, 0.0).then_inc(made, 1)
            gp.memset(zeros[:], 0.0).then_inc(made, 1)
            gp.memset(probs3[:], 0.0).then_inc(made, 1)
            gp.memset(ca_stack[:], 0.0).then_inc(made, 1)
            gp.memset(m_stack[:], 0.0).then_inc(made, 1)
            gp.memset(ca_rows[:].bitcast(U32), 0).then_inc(made, 1)

            def split(src, rest, parts, base, done):
                gp.tensor_tensor(parts[:, 0, :], src, zeros[:, :], ALU.add).then_inc(done, 1)
                pool.wait_ge(done, base + 1)
                gp.tensor_tensor(rest[:, :], src, parts[:, 0, :], ALU.subtract).then_inc(done, 1)
                pool.wait_ge(done, base + 2)
                gp.tensor_tensor(parts[:, 1, :], rest[:, :], zeros[:, :], ALU.add).then_inc(done, 1)
                pool.wait_ge(done, base + 3)

            pool.wait_ge(a_drained, RING_A.no("prologue", "caQ")[0] + 1)
            pool.wait_ge(made, 13)
            split(caQ[:, :], ca_rest, ca_parts, 0, ca_split)
            for slot, part in sorted(enumerate(CA_PART), key=lambda sp: -sp[1]):
                dst = ca_stack[:, :, :, T * slot:T * slot + T]
                if part == 2:
                    src, less = (t.rearrange("q (b t) -> q b t", t=T).unsqueeze(2)
                                 .broadcast_to([S, B, 4, T]) for t in (ca_rest[:, :], ca_parts[:, 1, :]))
                    gp.tensor_tensor(dst, src, less, ALU.subtract).then_inc(ca_split, 1)
                else:
                    src = ca_parts[:, part, :].rearrange("q (b t) -> q b t", t=T)
                    src = src.unsqueeze(2).broadcast_to([S, B, 4, T])
                    gp.tensor_copy(dst, src).then_inc(ca_split, 1)

            def stack_m(at):
                if at == "prologue":
                    base, filled = 0, RING_A.no(at, "MT")[0]
                else:
                    base, filled = at.lin(9, 9), RING_A.no(at, "MT")[0]
                pool.wait_ge(a_drained, filled + 1)
                if at != "prologue":
                    if at.kind == "first":
                        pool.wait_ge(d_filled, RING_D.no("prologue", "MsT")[0] + 1)
                    else:
                        pool.wait_ge(d_filled, RING_D.no(at, "ctxT")[0] + 1)
                split(m[:, :], m_rest, m_parts, base, m_step)
                for slot, part in sorted(enumerate(M_PART), key=lambda sp: -sp[1]):
                    dst = m_stack[:, :, :, T * slot:T * slot + T].rearrange("k b h t -> k (b h) t")
                    src = (m_rest[:, :] if part == 2 else m_parts[:, part, :]) \
                        .rearrange("k (bh t) -> k bh t", t=T)
                    if part == 2:
                        less = m_parts[:, 1, :].rearrange("k (bh t) -> k bh t", t=T)
                        gp.tensor_tensor(dst, src, less, ALU.subtract).then_inc(m_step, 1)
                    else:
                        gp.tensor_copy(dst, src).then_inc(m_step, 1)

            def add_bias(par):
                for b in range(2):
                    gp.tensor_tensor(xb[:, par, b, :], x_sb[:, par, b, 0:HID], bias[:, :],
                                     ALU.add).then_inc(xb_made, 1)

            pool.wait_ge(loaded_bias, 16)
            pool.wait_ge(loaded_x[0], 16)
            add_bias(0)
            stack_m("prologue")

            def body(at):
                if at.kind == "last":
                    return
                if at.kind != "first":
                    pool.wait_ge(d_drained, RING_D.no(at, "out1")[0] + 1)
                pool.wait_ge(loaded_x[1 - at.par], at.next().half(16, 16))
                add_bias(1 - at.par)
                stack_m(at)

            pairs(pool, body)

        @block.scalar
        def _(act):
            def copy(dst, src, scale=1.0):
                return nc.scalar.activation(dst, src, ACT.Copy, scale=scale)

            def piece(at, name):
                n, bank = RING_A.no(at, name)
                act.wait_ge(a_filled, n + 1)
                return bank_a[bank]

            act.wait_ge(made, 13)
            src = piece("prologue", "caQ")
            copy(caQ[:, :], src[:, 0:B * T]).then_inc(a_drained, 1)
            src = piece("prologue", "WcaT")
            copy(wca_t[:, :, :], src[0:KC, 0:NC * T].rearrange("p (c t) -> p c t", c=NC)) \
                .then_inc(a_drained, 1)
            for c in (0, 2):
                src = piece("prologue", f"WqT{c}")
                copy(wqT[:, c, :], src[0:KC, 0:PAD]).then_inc(a_drained, 1)
            src = piece("prologue", "k2T")
            for j in range(3):
                last = nc.scalar.activation(
                    k2_blocks[:, :, :, T * j:T * j + T],
                    src[0:KC, 0:NC * B * T].rearrange("p (c b t) -> p c b t", c=NC, b=B),
                    ACT.Copy, scale=hmask[:, 0, j, 0:1])
            last.then_inc(a_drained, 1)
            g_out(act, copy, piece("prologue", "G1"), 1).then_inc(a_drained, 1)
            for n in (0, 2):
                src = piece("prologue", f"VW{n}")
                copy(vw[:, n, :], src[:, 0:HID]).then_inc(a_drained, 1)
            src = piece("prologue", "CA1")
            ca_rows_out(copy, src, 1).then_inc(a_drained, 1)

            def front(at, name):
                par = 0 if at == "prologue" else 1 - at.par
                src = piece(at, name)
                if name == "xT01":
                    ins = copy(xT[:, 0:2, :], src[0:KC, :].rearrange("p (c n) -> p c n", c=2))
                elif name == "xT2":
                    ins = copy(xT[:, 2, :], src[0:KC, 0:2 * S])
                elif name == "MT":
                    if at != "prologue":
                        act.wait_ge(m_step, at.lin(9, 9))
                    ins = copy(m[:, :], src[:, 0:2 * HT], SCALE)
                elif name == "QT01":
                    ins = copy(qT[:, 0:2, :], src[0:KC, :].rearrange("p (c n) -> p c n", c=2), SCALE)
                elif name == "QT2":
                    ins = copy(qT[:, 2, :], src[0:KC, 0:2 * S], SCALE)
                else:
                    ins = copy(v_sb[0:KEYS, par, int(name[1]), :], src[0:KEYS, 0:HID])
                ins.then_inc(a_drained, 1)

            def turn_out(at, name, dst):
                src = piece(at, name)
                copy(dst, src[0:KC, 0:NC * S].rearrange("p (c n) -> p c n", c=NC)) \
                    .then_inc(a_drained, 1)

            def exps(n, par, keys):
                for half in range(2):
                    act.wait_ge(maxed, n * 2 + (half + 1))
                    for h in range(4 * half, 4 * half + 4):
                        k = h % 4
                        last = nc.scalar.activation(
                            probs[:, h, 0:keys], scores[half][:, k * keys:(k + 1) * keys], ACT.Exp,
                            bias=neg_max[:, h:h + 1], accum_out=sums[:, par, h:h + 1])
                    last.then_inc(exped, 1)

            for name in RING_A.lists["prologue"][len(SETUP_A):]:
                front("prologue", name)
            exps(0, 0, S)

            def body(at):
                more = at.kind != "last"
                if at.kind != "first":
                    turn_out(at, "hsT1", hsT[:, 1])
                if more:
                    front(at, "xT01")
                exps(unit(at, 1), 1, S)
                if more:
                    front(at, "xT2")
                    front(at, "MT")
                exps(unit(at, 2), 0, KEYS)
                turn_out(at, "hs1T0", hs1T[:, 0])
                turn_out(at, "hs1T1", hs1T[:, 1])
                exps(unit(at, 3), 1, KEYS)
                if more:
                    front(at, "QT01")
                    front(at, "V0")
                act.wait_ge(d_drained, RING_D.no(at, "sc3")[0] + 1)
                nc.scalar.activation(exp3[:], less3[:], ACT.Exp).then_inc(exp3_made, 1)
                if more:
                    front(at, "QT2")
                    exps(unit(at, 4), 0, S)
                    front(at, "V1")
                src = piece(at, "P3T")
                copy(probs3T[:, :, :], src[:, 0:2 * S].rearrange("p (b n) -> p b n", b=2)) \
                    .then_inc(a_drained, 1)
                turn_out(at, "hsT0", hsT[:, 0])

            pairs(act, body)
            turn_out("epilogue", "hsT1", hsT[:, 1])

        @block.vector
        def _(dve):
            v = nc.vector

            def copy(dst, src):
                return v.tensor_copy(dst, src)

            def piece(at, name):
                n, bank = RING_D.no(at, name)
                dve.wait_ge(d_filled, n + 1)
                return bank_d[bank]

            dve.wait_ge(loaded_ca, 16)
            v.tensor_copy(ca_sel[:, :].rearrange("r (n two) -> r n two", two=2),
                          ca_all[:, :].rearrange("r (n three) -> r n three", three=3)[:, :, 0:2]) \
                .then_inc(ca_picked, 1)
            dve.wait_ge(ca_picked, 1)
            v.tensor_copy(ca_sel[:, S - 1:S], ca_all[:, CAD - 1:CAD]).then_inc(ca_picked, 1)
            src = piece("prologue", "caT")
            copy(caT[:, :, :], src[0:CC, 0:2 * B * T].rearrange("p (c n) -> p c n", c=2)) \
                .then_inc(d_drained, 1)
            dve.wait_ge(made, 6)
            dve.wait_ge(a_drained, RING_A.no("prologue", "WcaT")[0] + 1)
            v.tensor_tensor(wca_blocks[:].rearrange("p c (h t) -> p c h t", h=HEADS),
                            wca_t[:].unsqueeze(2).broadcast_to([KC, NC, HEADS, T]),
                            hmask[:], ALU.mult).then_inc(wca_copied, 1)
            src = piece("prologue", "WqT1")
            copy(wqT[:, 1, :], src[0:KC, 0:PAD]).then_inc(d_drained, 1)
            src = piece("prologue", "v2T")
            for c in range(NC):
                last = v.tensor_tensor(
                    v2_blocks[:, c].rearrange("p b (h t) -> p b h t", h=HEADS),
                    src[0:KC, c * B * T:(c + 1) * B * T].rearrange("p (b t) -> p b t", b=B)
                        .unsqueeze(2).broadcast_to([KC, B, HEADS, T]),
                    hmask[:, c].unsqueeze(1).broadcast_to([KC, B, HEADS, T]), ALU.mult)
            last.then_inc(d_drained, 1)
            g_out(dve, lambda o, i, s: v.tensor_scalar(o, i, s, None, ALU.mult),
                  piece("prologue", "G0"), 0).then_inc(d_drained, 1)
            g_out(dve, lambda o, i, s: v.tensor_scalar(o, i, s, None, ALU.mult),
                  piece("prologue", "G2"), 2).then_inc(d_drained, 1)
            for n in (1, 3):
                src = piece("prologue", f"VW{n}")
                copy(vw[:, n, :], src[:, 0:HID]).then_inc(d_drained, 1)
            src = piece("prologue", "CA0")
            dve.wait_ge(made, 13)
            ca_rows_out(copy, src, 0).then_inc(d_drained, 1)

            def front(at, name):
                par = 0 if at == "prologue" else 1 - at.par
                src = piece(at, name)
                if name == "ctxT":
                    ins = copy(ctxT[:, :, :], src[0:CC, :].rearrange("p (c n) -> p c n", c=2))
                elif name == "KT01":
                    for j in range(3):
                        for c in range(2):
                            ins = v.tensor_scalar(
                                k_blocks[:, par, c, j],
                                src[0:KC, c * 2 * KEYS:(c + 1) * 2 * KEYS]
                                    .rearrange("p (b k) -> p b k", b=2),
                                hmask[:, 0, j, 0:1], None, ALU.mult)
                elif name == "KT2":
                    for j in (1, 2):
                        ins = v.tensor_scalar(
                            k_blocks[:, par, 2, j],
                            src[0:KC, 0:2 * KEYS].rearrange("p (b k) -> p b k", b=2),
                            hmask[:, 0, j, 0:1], None, ALU.mult)
                else:
                    ins = copy(m_rows[:, :, :, :],
                               src[:, 0:2 * S].bitcast(BF16)
                                   .rearrange("p (b g n) -> p b g n", b=2, g=2))
                ins.then_inc(d_drained, 1)

            def maxima(n, keys):
                for half in range(2):
                    dve.wait_ge(scored, n * 2 + (half + 1))
                    v.tensor_reduce(neg_max[:, 4 * half:4 * half + 4],
                                    scores[half][:, 0:4 * keys].rearrange("q (h k) -> q h k", h=4),
                                    AX.X, ALU.max, negate=True).then_inc(maxed, 1)

            def turned_copy(n, keys):
                for half in range(2):
                    dve.wait_ge(turned_full, n * 2 + (half + 1))
                    copy(probsT[0:keys, 4 * half:4 * half + 4, :],
                         turned[half][0:keys, :].rearrange("k (h q) -> k h q", h=4)) \
                        .then_inc(turned_out, 1)

            def norm(at, k):
                n = unit(at, k)
                dve.wait_ge(exped, n * 2 + 2)
                v.reciprocal(recip[:, k % 2, :], sums[:, k % 2, :]).then_inc(inverted, 1)
                src = piece(at, f"PV{k}")
                dve.wait_ge(inverted, n + 1)
                v.tensor_tensor(hs[:, k, 0:HID].rearrange("q (h d) -> q h d", h=HEADS),
                                src[:, 0:HID].rearrange("q (h d) -> q h d", h=HEADS),
                                recip[:, k % 2, :].unsqueeze(2).broadcast_to([S, HEADS, D]),
                                ALU.mult).then_inc(d_drained, 1)

            def finish(at, name, b, par, done):
                src = piece(at, name)
                if done is not None:
                    dve.wait_ge(stored[b], done)
                if at == "epilogue":
                    dve.wait_ge(xb_made, B)
                elif name == "out1":
                    dve.wait_ge(xb_made, at.lin(2))
                else:
                    dve.wait_ge(xb_made, at.lin(2, 1))
                v.tensor_tensor(out_sb[:, b, :], src[:, 0:HID], xb[:, par, b, :], ALU.add) \
                    .then_inc(d_drained, 1)

            for name in RING_D.lists["prologue"][len(SETUP_D):]:
                front("prologue", name)
            maxima(0, S)

            def body(at):
                more = at.kind != "last"
                turned_copy(unit(at, 0), S)
                maxima(unit(at, 1), S)
                if more:
                    front(at, "ctxT")
                if at.kind != "first":
                    finish(at, "out1", 1, 1 - at.par, None if at.a == 0 and at.b == 1
                           else at.lin(16, -16))
                norm(at, 0)
                turned_copy(unit(at, 1), S)
                maxima(unit(at, 2), KEYS)
                if more:
                    front(at, "KT01")
                    front(at, "KT2")
                norm(at, 1)
                turned_copy(unit(at, 2), KEYS)
                maxima(unit(at, 3), KEYS)
                src = piece(at, "sc3")[:, 0:2 * HT].rearrange("q (h t) -> q h t", t=T)
                v.tensor_reduce(max3[:], src, AX.X, ALU.max).then_inc(max3_made, 1)
                dve.wait_ge(max3_made, at.lin(1, 1))
                v.tensor_tensor(less3[:], src,
                                max3[:].unsqueeze(2).broadcast_to([S, 2 * HEADS, T]),
                                ALU.subtract).then_inc(d_drained, 1)
                norm(at, 2)
                turned_copy(unit(at, 3), KEYS)
                if more:
                    front(at, "MsT")
                dve.wait_ge(exp3_made, at.lin(1, 1))
                v.tensor_reduce(sum3[:, 0, :], exp3[:], AX.X, ALU.add).then_inc(sum3_made, 1)
                dve.wait_ge(sum3_made, at.lin(1, 1))
                v.reciprocal(sum3[:, 1, :], sum3[:, 0, :]).then_inc(inv3_made, 1)
                dve.wait_ge(inv3_made, at.lin(1, 1))
                for b in range(2):
                    v.tensor_tensor(
                        probs3[:, at.par, b, 2 * at.par + b].rearrange("q (h t) -> q h t", t=T),
                        exp3[:, HEADS * b:HEADS * (b + 1)],
                        sum3[:, 1, HEADS * b:HEADS * (b + 1)].unsqueeze(2)
                            .broadcast_to([S, HEADS, T]),
                        ALU.mult).then_inc(probs3_made, 1)
                if more:
                    maxima(unit(at, 4), S)
                norm(at, 3)
                finish(at, "out0", 0, at.par, None if at.kind == "first" else at.lin(16))

            pairs(dve, body)
            finish("epilogue", "out1", 1, (PAIRS - 1) % 2, 16 * (PAIRS - 1))

        @block.tensor
        def _(pe):
            mm = nc.tensor.matmul

            def fill_a(at, name):
                n, bank = RING_A.no(at, name)
                if not (isinstance(n, int) and n < 2):
                    pe.wait_ge(a_drained, n - 1)
                return bank_a[bank]

            def fill_d(at, name):
                n, bank = RING_D.no(at, name)
                if not (isinstance(n, int) and n < 2):
                    pe.wait_ge(d_drained, n - 1)
                return bank_d[bank]

            def got_a(at, name):
                pe.wait_ge(a_drained, RING_A.no(at, name)[0] + 1)

            def got_d(at, name):
                pe.wait_ge(d_drained, RING_D.no(at, name)[0] + 1)

            def turn(dst, src, rows, eye=None):
                return nc.tensor.transpose(dst, src, (ident if eye is None else eye)[0:rows, 0:rows])

            pe.wait_ge(made, 3)
            pe.wait_ge(loaded_ca, 16)
            dst = fill_d("prologue", "caT")
            for c in range(2):
                last = turn(dst[0:CC, c * B * T:(c + 1) * B * T], ca_all[:, c * CC:(c + 1) * CC], B * T)
            last.then_inc(d_filled, 1)
            pe.wait_ge(ca_picked, 2)
            dst = fill_a("prologue", "caQ")
            turn(dst[:, 0:B * T], ca_sel[:, :], B * T).then_inc(a_filled, 1)
            pe.wait_ge(zeroed, 6)
            pe.wait_ge(loaded_wqca, 16)
            dst = fill_a("prologue", "WcaT")
            for c in range(NC):
                last = turn(dst[0:KC, c * T:(c + 1) * T], wq_ca[:, c * KC:(c + 1) * KC], T)
            last.then_inc(a_filled, 1)
            pe.wait_ge(loaded_wq, 32)
            for c in range(NC):
                fill = fill_d if c == 1 else fill_a
                dst = fill("prologue", f"WqT{c}")
                for r in range(NC):
                    last = turn(dst[0:KC, r * KC:(r + 1) * KC], wq[:, r, c * KC:(c + 1) * KC], KC)
                last.then_inc(d_filled if c == 1 else a_filled, 1)
            pe.wait_ge(loaded_wca, 32)
            got_d("prologue", "caT")
            for w, fill, name, done in ((wk_ca, fill_a, "k2T", a_filled), (wv_ca, fill_d, "v2T", d_filled)):
                dst = fill("prologue", name)
                for c in range(NC):
                    for r in range(2):
                        last = mm(dst[0:KC, c * B * T:(c + 1) * B * T], w[:, r, c * KC:(c + 1) * KC],
                                  caT[:, r, :], start=r == 0, stop=r == 1)
                last.then_inc(done, 1)
            got_a("prologue", "k2T")
            got_d("prologue", "WqT1")
            for r in range(NC):
                fill = fill_a if r == 1 else fill_d
                dst = fill("prologue", f"G{r}")
                for c in range(NC):
                    heads = 3 if c < 2 else 2
                    width = B * heads * T
                    last = mm(dst[0:KC, c * B * 3 * T:c * B * 3 * T + width],
                              wqT[:, c, r * KC:(r + 1) * KC], k2_blocks[:, c, :, 0:heads * T],
                              start=True, stop=True)
                last.then_inc(a_filled if r == 1 else d_filled, 1)
            pe.wait_ge(loaded_wout, 32)
            got_d("prologue", "v2T")
            for n in range(4):
                fill = fill_d if n % 2 else fill_a
                dst = fill("prologue", f"VW{n}")
                for c in range(NC):
                    last = mm(dst[:, 0:HID],
                              v2_blocks[:, c, 4 * n:4 * n + 4, :].rearrange("p b n -> p (b n)"),
                              wout[:, c, :], start=c == 0, stop=c == NC - 1)
                last.then_inc(d_filled if n % 2 else a_filled, 1)
            pe.wait_ge(ca_split, 3 + len(CA_PART))
            for n in range(2):
                dst = (fill_a if n else fill_d)("prologue", f"CA{n}").bitcast(BF16)
                for b in range(8):
                    last = turn(dst[:, b * S:(b + 1) * S],
                                ca_stack[:, 8 * n + b].rearrange("q j n -> q (j n)"), S, ident16)
                last.then_inc(a_filled if n else d_filled, 1)

            def front(at, name):
                par = 0 if at == "prologue" else 1 - at.par
                seen = 16 if at == "prologue" else at.next().half(16, 16)
                a = name in RING_A.lists["prologue"]
                dst = (fill_a if a else fill_d)(at, name)
                if name in ("xT01", "xT2"):
                    if name == "xT01":
                        pe.wait_ge(loaded_x[par], seen)
                    for i, c in enumerate((0, 1) if name == "xT01" else (2,)):
                        for b in range(2):
                            last = turn(dst[0:KC, (2 * i + b) * S:(2 * i + b + 1) * S],
                                        x_sb[:, par, b, c * KC:(c + 1) * KC], S)
                elif name == "ctxT":
                    pe.wait_ge(loaded_ctx[par], seen)
                    for c in range(2):
                        for b in range(2):
                            last = turn(dst[0:CC, (2 * c + b) * S:(2 * c + b + 1) * S],
                                        ctx_sb[:, par, b, c * CC:(c + 1) * CC], S)
                elif name == "MT":
                    got_a(at, "xT2")
                    for b in range(2):
                        for c in range(NC):
                            last = mm(dst[:, b * HT:(b + 1) * HT], xT[:, c, b * S:(b + 1) * S],
                                      wca_blocks[:, c, :], start=c == 0, stop=c == NC - 1)
                elif name in ("QT01", "QT2"):
                    for i, c in enumerate((0, 1) if name == "QT01" else (2,)):
                        for r in range(NC):
                            last = mm(dst[0:KC, i * 2 * S:(i + 1) * 2 * S],
                                      wq[:, r, Q_COLS[c]:Q_COLS[c] + KC], xT[:, r, :],
                                      start=r == 0, stop=r == NC - 1)
                elif name in ("KT01", "KT2"):
                    got_d(at, "ctxT")
                    for i, c in enumerate((0, 1) if name == "KT01" else (2,)):
                        for r in range(2):
                            last = mm(dst[0:KC, i * 2 * KEYS:(i + 1) * 2 * KEYS],
                                      wk[:, r, Q_COLS[c]:Q_COLS[c] + KC],
                                      ctxT[:, r, :].rearrange("p (b k) -> p b k", b=2)[:, :, 0:KEYS],
                                      start=r == 0, stop=r == 1)
                elif name in ("V0", "V1"):
                    b = int(name[1])
                    for r in range(2):
                        last = mm(dst[0:KEYS, 0:HID], ctxT[:, r, b * S:b * S + KEYS], wv[:, r, :],
                                  start=r == 0, stop=r == 1)
                else:
                    pe.wait_ge(m_step, 9 if at == "prologue" else at.lin(9, 18))
                    dst = dst.bitcast(BF16)
                    for b in range(2):
                        for k in range(2):
                            last = turn(dst[:, (2 * b + k) * S:(2 * b + k + 1) * S],
                                        m_stack[:, b, 4 * k:4 * k + 4, :]
                                            .rearrange("q h n -> q (h n)"), S, ident16)
                last.then_inc(a_filled if a else d_filled, 1)

            def channel_scores(n, at, b):
                row = at.lin(2, b)
                for half in range(2):
                    for k in range(4):
                        last = mm(scores[half][:, k * S:(k + 1) * S],
                                  ca_rows[:, bass.ds(row, 1), k, :].rearrange("p b q -> p (b q)"),
                                  m_rows[:, b, half, :], start=True, stop=True)
                    last.then_inc(scored, 1)

            def token_scores(at, b):
                tok = slice(b * S, (b + 1) * S)
                for half, runs in enumerate((((0, 0, 3), (1, 0, 1)), ((1, 1, 2), (2, 1, 2)))):
                    col = 0
                    for c, j, heads in runs:
                        width = heads * KEYS
                        last = mm(scores[half][:, col:col + width], qT[:, c, tok],
                                  k_blocks[:, at.par, c, j:j + heads, b, :], start=True, stop=True)
                        col += width
                    last.then_inc(scored, 1)

            def turn_probs(n, keys):
                for half in range(2):
                    pe.wait_ge(exped, n * 2 + (half + 1))
                    for k in range(4):
                        last = turn(turned[half][0:keys, k * S:(k + 1) * S],
                                    probs[:, 4 * half + k, 0:keys], S)
                    last.then_inc(turned_full, 1)

            def weigh(at, k):
                n, b, keys = unit(at, k), k % 2, S if k < 2 else KEYS
                values = x_sb if k < 2 else v_sb
                dst = fill_d(at, f"PV{k}")
                pe.wait_ge(turned_out, n * 2 + 2)
                for h in range(HEADS):
                    last = mm(dst[:, h * D:(h + 1) * D], probsT[0:keys, h, :],
                              values[0:keys, at.par, b, h * D:(h + 1) * D], start=True, stop=True)
                last.then_inc(d_filled, 1)

            def turn_hidden(at, name, k, after):
                dst = fill_a(at, name)
                pe.wait_ge(d_drained, after + 1)
                for c in range(NC):
                    last = turn(dst[0:KC, c * S:(c + 1) * S], hs[:, k, c * KC:(c + 1) * KC], S)
                last.then_inc(a_filled, 1)

            def project(at, name, b, group):
                dst = fill_d(at, name)
                got_a(at, f"hsT{b}")
                for c in range(NC):
                    mm(dst[:, 0:HID], hsT[:, b, c, :], wout[:, c, :], start=c == 0, stop=False)
                mm(dst[:, 0:HID], probs3T[:, b, :],
                   vw[:, bass.ds(group, 1), :].rearrange("p g n -> p (g n)"),
                   start=False, stop=True).then_inc(d_filled, 1)

            pe.wait_ge(made, 13)
            order = ["xT01", "xT2", "ctxT", "MT", "KT01", "KT2", "QT01", "V0", "QT2", "V1", "MsT"]
            for name in order:
                if name == "MT":
                    pe.wait_ge(wca_copied, 1)
                if name == "KT01":
                    pe.wait_ge(loaded_wkv, 32)
                front("prologue", name)
            got_a("prologue", "CA1")
            got_d("prologue", "MsT")
            channel_scores(0, At(0, 0, 0, "first"), 0)

            def body(at):
                more = at.kind != "last"
                turn_probs(unit(at, 0), S)
                channel_scores(unit(at, 1), at, 1)
                if at.kind != "first":
                    prev = RING_D.no(at, "ctxT" if more else "out1")[0] - 2
                    turn_hidden(at, "hsT1", 3, prev)
                if more:
                    front(at, "xT01")
                    front(at, "xT2")
                    front(at, "ctxT")
                if at.kind != "first":
                    project(at, "out1", 1, at.half(1) if at.par else at.half(1, -1))
                weigh(at, 0)
                turn_probs(unit(at, 1), S)
                if at.kind == "first":
                    got_a("prologue", "QT2")
                token_scores(at, 0)
                if more:
                    front(at, "MT")
                    front(at, "KT01")
                    front(at, "KT2")
                weigh(at, 1)
                turn_hidden(at, "hs1T0", 0, RING_D.no(at, "PV0")[0])
                turn_probs(unit(at, 2), KEYS)
                token_scores(at, 1)
                turn_hidden(at, "hs1T1", 1, RING_D.no(at, "PV1")[0])
                if more:
                    front(at, "QT01")
                    front(at, "V0")
                dst = fill_d(at, "sc3")
                got_a(at, "hs1T1")
                for b in range(2):
                    for c in range(NC):
                        last = mm(dst[:, b * HT:(b + 1) * HT], hs1T[:, b, c, :],
                                  g[:, c, bass.ds(at.lin(2, b), 1), :].rearrange("p b n -> p (b n)"),
                                  start=c == 0, stop=c == NC - 1)
                last.then_inc(d_filled, 1)
                weigh(at, 2)
                turn_probs(unit(at, 3), KEYS)
                if more:
                    front(at, "MsT")
                    got_d(at, "MsT")
                    channel_scores(unit(at, 4), at.next(), 0)
                    front(at, "QT2")
                    front(at, "V1")
                weigh(at, 3)
                dst = fill_a(at, "P3T")
                pe.wait_ge(probs3_made, at.lin(2, 2))
                for b in range(2):
                    last = turn(dst[:, b * S:(b + 1) * S],
                                probs3[:, at.par, b].rearrange("q j n -> q (j n)"), S)
                last.then_inc(a_filled, 1)
                turn_hidden(at, "hsT0", 2, RING_D.no(at, "PV2")[0])
                project(at, "out0", 0, at.half(1))

            pairs(pe, body)
            turn_hidden("epilogue", "hsT1", 3, RING_D.no("epilogue", "out1")[0] - 2)
            project("epilogue", "out1", 1, (PAIRS - 1) // 2)


_INS = ['x', 'ctx_768', 'L0_xattn_Wq', 'L0_xattn_Wk', 'L0_xattn_Wv', 'L0_xattn_Wq_ca', 'L0_xattn_Wk_ca',
        'L0_xattn_Wv_ca', 'L0_xattn_Wout', 'L0_xattn_b_out']


def kernel(**inputs):
    import numpy as np
    import concourse.bacc as bacc
    from concourse import mybir as mb
    from concourse.bass_utils import run_bass_kernel_spmd

    nc = bacc.Bacc("TRN2", target_bir_lowering=False, num_devices=1)
    arrays, args = {}, []
    for name in _INS:
        a = np.ascontiguousarray(inputs[name])
        arrays[f"in_{name}"] = a
        args.append(nc.dram_tensor(f"in_{name}", a.shape, mb.dt.from_np(a.dtype), kind="ExternalInput").ap())
    args.append(nc.dram_tensor("out_0", (B, S, HID), mb.dt.float32, kind="ExternalOutput").ap())
    attention(nc, *args)
    r = run_bass_kernel_spmd(nc, [arrays], core_ids=[0])
    return r.results[0]["out_0"]
```

```python
from contextlib import ExitStack

import concourse.bass as bass
from concourse import mybir

F32 = mybir.dt.float32
F32R = mybir.dt.float32r
BF16 = mybir.dt.bfloat16
U32 = mybir.dt.uint32
ACT = mybir.ActivationFunctionType
ALU = mybir.AluOpType
AX = mybir.AxisListType

B, S, HID = 16, 128, 320
CAD, T = 192, 4
HEADS = 8
D = HID // HEADS
SCALE = float(D) ** -0.5
KEYS = S - T
PAIRS = B // 2
KC = 3 * D
NC = 3
PAD = KC * NC
CC = CAD // 2
HT = HEADS * T
QC = 6 * D
QW = HID + HT
Q_CHUNKS = [slice(0, KC), slice(KC, QC), slice(QC, QW)]
KL = QW - QC
M_PART = [0, 0, 0, 1, 1, 2]
CA_PART = [0, 1, 2, 0, 1, 0]


class At:

    def __init__(self, j, a, b, kind):
        self.j, self.a, self.b, self.kind = j, a, b, kind
        self.par = b % 2

    def lin(self, per, off=0):
        if self.a == 0:
            return per * self.b + off
        return self.j * (per * self.a) + (per * self.b + off)

    def half(self, per, off=0):
        if self.a == 0:
            return per * (self.b // 2) + off
        return self.j * per + (per * (self.b // 2) + off)

    def next(self):
        return At(self.j, self.a, self.b + 1, "next")


class Ring:

    def __init__(self, prologue, first, mid, last, epilogue):
        self.lists = dict(prologue=prologue, first=first, mid=mid, last=last, epilogue=epilogue)

    def no(self, at, name):
        n = {k: len(v) for k, v in self.lists.items()}
        if at == "prologue":
            k = self.lists["prologue"].index(name)
            return k, k % 2
        if at == "epilogue":
            k = n["prologue"] + n["first"] + (PAIRS - 2) * n["mid"] + n["last"]
            k += self.lists["epilogue"].index(name)
            return k, k % 2
        k = self.lists[at.kind].index(name)
        if at.kind == "first":
            k += n["prologue"]
            return k, k % 2
        k += n["prologue"] + n["first"] - n["mid"]
        return at.lin(n["mid"], k), (n["mid"] * at.b + k) % 2


LATE_A = [["k2T", "WqT0", "WqT2"], ["G1"], ["VW0"], ["VW2", "CA1"]]
LATE_D = [["caT", "v2T", "WqT1"], ["G0", "G2"], ["VW1"], ["VW3"]]


def of_a(late, end, front):
    return (end * ["P3T", "hsT0", "hsT1"] + front * ["xT01", "xT2"] + late * LATE_A[0]
            + late * LATE_A[1] + front * ["QM", "MT"] + ["hs1T0", "hs1T1"]
            + late * LATE_A[2] + front * ["QT01"] + late * LATE_A[3] + front * ["V0", "V1"])


def of_d(late, end, front):
    return (front * ["ctxT"] + late * LATE_D[0] + ["PV0"] + end * ["out0"]
            + late * LATE_D[1] + front * ["KT2"] + end * ["out1"] + ["PV1"]
            + front * ["KT01"] + late * LATE_D[2] + front * ["MsT"] + ["PV2"]
            + late * LATE_D[3] + ["sc3", "PV3"])


LATE_ORDER = ["caT", "k2T", "v2T", "WqT0", "WqT1", "WqT2", "G0", "G1", "G2",
              "VW0", "VW1", "VW2", "VW3", "CA1"]
RING_A = Ring(["caQ", "WcaT", "xT01", "xT2", "QM", "MT", "QT01", "V0", "V1"],
              of_a(1, 0, 1), of_a(0, 1, 1), of_a(0, 1, 0), ["P3T", "hsT0", "hsT1"])
RING_D = Ring(["ctxT", "KT2", "KT01", "CA0", "MsT"],
              of_d(1, 0, 1), of_d(0, 1, 1), of_d(0, 1, 0), ["out0", "out1"])


def attention(nc, x, ctx, Wq, Wk, Wv, Wq_ca, Wk_ca, Wv_ca, Wout, b_out, out):
    with ExitStack() as stack:
        def sb(name, shape, dt=F32):
            return stack.enter_context(nc.sbuf_tensor(name, shape, dt))

        def ps(name, dt=F32):
            return stack.enter_context(nc.psum_tensor(name, [128, 512], dt))

        def sem(name):
            return stack.enter_context(nc.semaphore(name))

        wq = sb("wq", [KC, NC, QW])
        wk = sb("wk", [CC, 2, QW])
        wv = sb("wv", [CC, 2, HID])
        wk_ca = sb("wk_ca", [CC, 2, PAD])
        wv_ca = sb("wv_ca", [CC, 2, PAD])
        wout = sb("wout", [KC, NC, HID])
        wq_ca = sb("wq_ca", [T, PAD])
        wq_r = [sb(f"wq_r{i}", [KC, NC, QW], F32R) for i in range(2)]
        wk_r = [sb(f"wk_r{i}", [CC, 2, QW], F32R) for i in range(2)]
        wv_r = [sb(f"wv_r{i}", [CC, 2, HID], F32R) for i in range(2)]
        wout_r = [sb(f"wout_r{i}", [KC, NC, HID], F32R) for i in range(2)]
        bias = sb("bias", [128, HID])
        ident = sb("ident", [128, 128])
        ident16 = sb("ident16", [128, 128], BF16)
        zeros = sb("zeros", [128, 2 * 2 * S])
        last_mask = sb("last_mask", [KL, 2])
        hmask = sb("hmask", [KC, NC, HEADS, T])
        ca_all = sb("ca_all", [B * T, CAD])
        ca_sel = sb("ca_sel", [B * T, S])
        caT = sb("caT", [CC, 2, B * T])
        caQ = sb("caQ", [S, B * T])
        ca_rest = sb("ca_rest", [S, B * T])
        ca_parts = sb("ca_parts", [S, 2, B * T], BF16)
        ca_stack = sb("ca_stack", [S, B, 4, 32], BF16)
        ca_rows = sb("ca_rows", [128, B, 4, S], BF16)
        wca_t = sb("wca_t", [KC, NC, T])
        wqT = sb("wqT", [KC, NC, PAD])
        k2_blocks = sb("k2_blocks", [KC, NC, B, 3 * T])
        v2_blocks = sb("v2_blocks", [KC, NC, B, HT])
        g = sb("g", [KC, NC, B, HT])
        vw = sb("vw", [128, B // 4, HID])
        x_sb = sb("x_sb", [S, 2, 2, PAD])
        ctx_sb = sb("ctx_sb", [S, 2, 2, CAD])
        xb = sb("xb", [S, 2, 2, HID])
        xT = sb("xT", [KC, NC, 2 * S])
        ctxT = sb("ctxT", [CC, 2, 2 * S])
        xT_r = [sb(f"xT_r{i}", [KC, NC, 2 * S], F32R) for i in range(2)]
        ctxT_r = [sb(f"ctxT_r{i}", [CC, 2, 2 * S], F32R) for i in range(2)]
        qT = sb("qT", [KC, 2, NC, 2 * S])
        k_blocks = sb("k_blocks", [KC, 2, NC, 3, 2, KEYS])
        v_sb = sb("v_sb", [S, 2, 2, HID])
        m = sb("m", [S, 2 * HT])
        m_rest = sb("m_rest", [S, 2 * HT])
        m_parts = sb("m_parts", [S, 2, 2 * HT], BF16)
        m_stack = sb("m_stack", [S, 2, HEADS, 32], BF16)
        m_rows = sb("m_rows", [128, 2, 2, S], BF16)
        neg_max = sb("neg_max", [S, HEADS])
        probs = sb("probs", [S, HEADS, S])
        sums = sb("sums", [S, 2, HEADS])
        recip = sb("recip", [S, 2, HEADS])
        probsT = sb("probsT", [S, HEADS, S])
        hs = sb("hs", [S, 4, PAD])
        hs1T = sb("hs1T", [KC, 2, NC, S])
        hsT = sb("hsT", [KC, 2, NC, S])
        hsT_r = [sb(f"hsT_r{i}", [KC, 2, NC, S], F32R) for i in range(2)]
        max3 = sb("max3", [S, 2 * HEADS])
        less3 = sb("less3", [S, 2 * HEADS, T])
        exp3 = sb("exp3", [S, 2 * HEADS, T])
        sum3 = sb("sum3", [S, 2, 2 * HEADS])
        probs3 = sb("probs3", [S, 2, 2, 4, HT])
        probs3T = sb("probs3T", [128, 2, S])
        out_sb = sb("out_sb", [S, 2, HID])

        scores = [ps("scores0"), ps("scores1")]
        turned = [ps("turned0"), ps("turned1")]
        bank_a = [ps("bank_a0"), ps("bank_a1")]
        bank_d = [ps("bank_d0"), ps("bank_d1")]

        loaded_wqca = sem("loaded_wqca")
        loaded_ca = sem("loaded_ca")
        loaded_wq = sem("loaded_wq")
        loaded_wca = sem("loaded_wca")
        loaded_wout = sem("loaded_wout")
        loaded_wkv = sem("loaded_wkv")
        loaded_bias = sem("loaded_bias")
        loaded_x = [sem("loaded_x0"), sem("loaded_x1")]
        loaded_ctx = [sem("loaded_ctx0"), sem("loaded_ctx1")]
        out_free = [sem("out_free0"), sem("out_free1")]
        zeroed = sem("zeroed")
        made = sem("made")
        ca_zeroed = sem("ca_zeroed")
        ca_split = sem("ca_split")
        w_high = sem("w_high")
        w_low = sem("w_low")
        ctx_split = sem("ctx_split")
        x_split = sem("x_split")
        hs_split = sem("hs_split")
        m_step = sem("m_step")
        xb_made = sem("xb_made")
        ca_picked = sem("ca_picked")
        wca_copied = sem("wca_copied")
        a_filled = sem("a_filled")
        a_drained = sem("a_drained")
        d_filled = sem("d_filled")
        d_drained = sem("d_drained")
        scored = sem("scored")
        maxed = sem("maxed")
        exped = sem("exped")
        turned_full = sem("turned_full")
        turned_out = sem("turned_out")
        inverted = sem("inverted")
        max3_made = sem("max3_made")
        exp3_made = sem("exp3_made")
        sum3_made = sem("sum3_made")
        inv3_made = sem("inv3_made")
        probs3_made = sem("probs3_made")

        def g_out(engine, scaled, src, r):
            for c in range(NC):
                heads = 3 if c < 2 else 2
                last = scaled(g[:, r, :, 3 * T * c:3 * T * c + heads * T],
                              src[0:KC, c * B * 3 * T:c * B * 3 * T + B * heads * T]
                                  .rearrange("p (b n) -> p b n", b=B), SCALE)
            return last

        def ca_rows_out(copy, src, n):
            for j in range(4):
                last = copy(ca_rows[32 * j:32 * j + 32, 8 * n:8 * n + 8, j, :],
                            src[32 * j:32 * j + 32, :].bitcast(BF16)
                                .rearrange("p (b q) -> p b q", b=8))
            return last

        block = stack.enter_context(nc.Block())

        def pairs(engine, body):
            body(At(0, 0, 0, "first"))
            with engine.Fori(0, (PAIRS - 2) // 2) as j:
                body(At(j, 2, 1, "mid"))
                body(At(j, 2, 2, "mid"))
            body(At(0, 0, PAIRS - 1, "last"))

        def unit(at, k):
            return at.lin(4, k)

        @block.sync
        def _(sp):
            def load_pair(row, par):
                sp.dma_start(x_sb[:, par, :, 0:HID], x[bass.ds(row, 2)].rearrange("b s h -> s b h")) \
                    .then_inc(loaded_x[par], 16)
                sp.dma_start(ctx_sb[:, par, :, :], ctx[bass.ds(row, 2)].rearrange("b s h -> s b h")) \
                    .then_inc(loaded_ctx[par], 16)

            def store(b, row):
                sp.dma_start(out[bass.ds(row, 1)].rearrange("b s h -> (b s) h"), out_sb[:, b, :]) \
                    .then_inc(out_free[b], 16)

            load_pair(0, 0)
            sp.dma_start(ca_all[:, 0:CAD], ctx[:, KEYS:S, :]).then_inc(loaded_ca, 16)
            sp.dma_start(wq_ca[:, 0:HID], Wq_ca).then_inc(loaded_wqca, 16)
            sp.dma_start(bias[:, :], b_out.partition_broadcast(128)).then_inc(loaded_bias, 16)
            for w2, w2_sb in ((Wk_ca, wk_ca), (Wv_ca, wv_ca)):
                sp.dma_start(w2_sb[:, :, 0:HID], w2.rearrange("(c p) n -> p c n", p=CC)) \
                    .then_inc(loaded_wca, 16)
            load_pair(2, 1)
            sp.wait_ge(zeroed, 2)
            sp.dma_start(wout[:, 0:2, :], Wout[0:2 * KC, :].rearrange("(c p) n -> p c n", p=KC)) \
                .then_inc(loaded_wout, 16)
            sp.dma_start(wout[0:HID - 2 * KC, 2, :], Wout[2 * KC:HID, :]).then_inc(loaded_wout, 16)

            def fixed(value):
                return value if isinstance(value, int) else sp.snap(value)

            def body(at):
                loads = at.kind != "last" and not (at.a == 0 and at.b + 2 >= PAIRS)
                if at.kind != "first":
                    before = [fixed(at.lin(2, b - 2)) for b in range(2)]
                    out_made = [fixed(RING_D.no(at, f"out{b}")[0] + 1) for b in range(2)]
                if loads:
                    ahead = fixed(at.lin(2, 4))
                    x_used = fixed(RING_D.no(at, "PV1")[0] + 1)
                if at.kind != "first":
                    for b in range(2):
                        sp.wait_ge(d_drained, out_made[b])
                        store(b, before[b])
                if loads:
                    sp.wait_ge(d_filled, x_used)
                    load_pair(ahead, at.par)

            body(At(0, 0, 0, "first"))
            with sp.Fori(0, (PAIRS - 2) // 2 - 1) as j:
                body(At(j, 2, 1, "mid"))
                body(At(j, 2, 2, "mid"))
            body(At(0, 0, PAIRS - 3, "mid"))
            body(At(0, 0, PAIRS - 2, "mid"))
            body(At(0, 0, PAIRS - 1, "last"))
            for b in range(2):
                sp.wait_ge(d_drained, RING_D.no("epilogue", f"out{b}")[0] + 1)
                store(b, B - 2 + b)
            for b in range(2):
                sp.wait_ge(out_free[b], 16 * (PAIRS + 1))

        @block.gpsimd
        def _(pool):
            gp = nc.gpsimd
            gp.memset(wq[:, 2, :], 0.0).then_inc(zeroed, 1)
            gp.memset(wout[:, 2, :], 0.0).then_inc(zeroed, 1)
            gp.memset(wk[:, :, QC:QC + HT], 0.0).then_inc(zeroed, 1)
            gp.memset(wq_ca[:, HID:PAD], 0.0).then_inc(zeroed, 1)
            gp.memset(x_sb[:, :, :, HID:PAD], 0.0).then_inc(zeroed, 1)
            gp.memset(ident[:], 0.0).then_inc(made, 1)
            pool.wait_ge(made, 1)
            gp.affine_select(out=ident[:], in_=ident[:], compare_op=ALU.not_equal, fill=1.0, base=0,
                             pattern=[[-1, 128]], channel_multiplier=1).then_inc(made, 1)
            gp.memset(hmask[:], 1.0).then_inc(made, 1)
            pool.wait_ge(made, 3)
            gp.affine_select(out=hmask[:], in_=hmask[:], compare_op=ALU.is_ge, fill=0.0, base=0,
                             pattern=[[KC, NC], [-D, HEADS], [0, T]], channel_multiplier=1) \
                .then_inc(made, 1)
            pool.wait_ge(made, 4)
            gp.affine_select(out=hmask[:], in_=hmask[:], compare_op=ALU.is_ge, fill=0.0, base=D - 1,
                             pattern=[[-KC, NC], [D, HEADS], [0, T]], channel_multiplier=-1) \
                .then_inc(made, 1)
            gp.memset(zeros[:], 0.0).then_inc(made, 1)
            gp.memset(last_mask[:], 1.0).then_inc(made, 1)
            pool.wait_ge(made, 7)
            gp.affine_select(out=last_mask[:], in_=last_mask[:], compare_op=ALU.is_ge, fill=0.0,
                             base=-HT, pattern=[[-D, 2]], channel_multiplier=1).then_inc(made, 1)
            pool.wait_ge(made, 8)
            gp.affine_select(out=last_mask[:], in_=last_mask[:], compare_op=ALU.is_ge, fill=0.0,
                             base=HT + D - 1, pattern=[[D, 2]], channel_multiplier=-1) \
                .then_inc(made, 1)
            gp.memset(m_stack[:, :, :, T * len(M_PART):], 0.0).then_inc(made, 1)
            gp.tensor_copy(ident16[:], ident[:]).then_inc(made, 1)
            for b in range(2):
                gp.memset(out_sb[:, b, 0:2], 0.0).then_inc(out_free[b], 16)
            for t in (hs[:, :, HID:PAD], wk_ca[:, :, HID:PAD], wv_ca[:, :, HID:PAD], probs3[:]):
                gp.memset(t, 0.0).then_inc(made, 1)

            def split(src, rest, parts, base, done):
                gp.tensor_tensor(parts[:, 0, :], src, zeros[:, 0:2 * HT], ALU.add).then_inc(done, 1)
                pool.wait_ge(done, base + 1)
                gp.tensor_tensor(rest[:, :], src, parts[:, 0, :], ALU.subtract).then_inc(done, 1)
                pool.wait_ge(done, base + 2)
                gp.tensor_tensor(parts[:, 1, :], rest[:, :], zeros[:, 0:2 * HT], ALU.add) \
                    .then_inc(done, 1)
                pool.wait_ge(done, base + 3)

            def split_r(src, parts, base, done):
                rows, n = src.shape[0], src.shape[1]
                gp.tensor_tensor(parts[0], src, zeros[0:rows, 0:n], ALU.add).then_inc(done, 1)
                pool.wait_ge(done, base + 1)
                gp.tensor_tensor(parts[1], src, parts[0], ALU.subtract).then_inc(done, 1)

            def split_front(at):
                n = (lambda per: 0) if at == "prologue" else (lambda per: at.lin(per, per))
                pool.wait_ge(d_drained, RING_D.no(at, "ctxT")[0] + 1)
                split_r(ctxT[:].rearrange("p c n -> p (c n)"),
                        [t[:].rearrange("p c n -> p (c n)") for t in ctxT_r], n(2), ctx_split)
                for i, (piece, c) in enumerate((("xT01", slice(0, 2)), ("xT2", slice(2, 3)))):
                    pool.wait_ge(a_drained, RING_A.no(at, piece)[0] + 1)
                    split_r(xT[:, c].rearrange("p c n -> p (c n)"),
                            [t[:, c].rearrange("p c n -> p (c n)") for t in xT_r],
                            n(4) + 2 * i, x_split)

            def stack_m(at):
                if at == "prologue":
                    base, filled = 0, RING_A.no(at, "MT")[0]
                else:
                    base, filled = at.lin(9, 9), RING_A.no(at, "MT")[0]
                pool.wait_ge(a_drained, filled + 1)
                split(m[:, :], m_rest, m_parts, base, m_step)
                for slot, part in sorted(enumerate(M_PART), key=lambda sp: -sp[1]):
                    dst = m_stack[:, :, :, T * slot:T * slot + T].rearrange("k b h t -> k (b h) t")
                    src = (m_rest[:, :] if part == 2 else m_parts[:, part, :]) \
                        .rearrange("k (bh t) -> k bh t", t=T)
                    if part == 2:
                        less = m_parts[:, 1, :].rearrange("k (bh t) -> k bh t", t=T)
                        gp.tensor_tensor(dst, src, less, ALU.subtract).then_inc(m_step, 1)
                    else:
                        gp.tensor_copy(dst, src).then_inc(m_step, 1)

            def add_bias(par):
                for b in range(2):
                    gp.tensor_tensor(xb[:, par, b, :], x_sb[:, par, b, 0:HID], bias[:, :],
                                     ALU.add).then_inc(xb_made, 1)

            split_front("prologue")
            pool.wait_ge(loaded_bias, 16)
            pool.wait_ge(loaded_x[0], 16)
            add_bias(0)
            stack_m("prologue")

            def body(at):
                if at.kind == "last":
                    return
                split_front(at)
                if at.kind != "first":
                    pool.wait_ge(d_drained, RING_D.no(at, "out1")[0] + 1)
                pool.wait_ge(loaded_x[1 - at.par], at.next().half(16, 16))
                add_bias(1 - at.par)
                stack_m(at)

            pairs(pool, body)

        @block.scalar
        def _(act):
            def copy(dst, src, scale=1.0):
                return nc.scalar.activation(dst, src, ACT.Copy, scale=scale)

            def piece(at, name):
                n, bank = RING_A.no(at, name)
                act.wait_ge(a_filled, n + 1)
                return bank_a[bank]

            def high(dst, src, n):
                copy(dst[0][:], src[:]).then_inc(w_high, 1)

            act.wait_ge(zeroed, 3)
            act.dma_start(wq[:, 0:2, 0:QC], Wq[0:2 * KC, 0:QC].rearrange("(c p) n -> p c n", p=KC)) \
                .then_inc(loaded_wq, 16)
            act.dma_start(wq[:, 0:2, QC + HT:QW],
                          Wq[0:2 * KC, QC:HID].rearrange("(c p) n -> p c n", p=KC)) \
                .then_inc(loaded_wq, 16)
            act.dma_start(wq[0:HID - 2 * KC, 2, 0:QC], Wq[2 * KC:HID, 0:QC]).then_inc(loaded_wq, 16)
            act.dma_start(wq[0:HID - 2 * KC, 2, QC + HT:QW], Wq[2 * KC:HID, QC:HID]) \
                .then_inc(loaded_wq, 16)
            act.dma_start(wk[:, :, 0:QC], Wk[:, 0:QC].rearrange("(c p) n -> p c n", p=CC)) \
                .then_inc(loaded_wkv, 16)
            act.dma_start(wk[:, :, QC + HT:QW], Wk[:, QC:HID].rearrange("(c p) n -> p c n", p=CC)) \
                .then_inc(loaded_wkv, 16)
            act.dma_start(wv[:, :, :], Wv.rearrange("(c p) n -> p c n", p=CC)).then_inc(loaded_wkv, 16)
            src = piece("prologue", "caQ")
            copy(caQ[:, :], src[:, 0:B * T]).then_inc(a_drained, 1)
            src = piece("prologue", "WcaT")
            copy(wca_t[:, :, :], src[0:KC, 0:NC * T].rearrange("p (c t) -> p c t", c=NC)) \
                .then_inc(a_drained, 1)

            def late(at, step):
                for name in LATE_A[step]:
                    src = piece(at, name)
                    if name[:3] == "WqT":
                        c = int(name[3])
                        rows = KC if c < 2 else HID - 2 * KC
                        ins = copy(wqT[0:rows, c, :], src[0:rows, 0:PAD])
                    elif name == "k2T":
                        for j in range(3):
                            ins = nc.scalar.activation(
                                k2_blocks[:, :, :, T * j:T * j + T],
                                src[0:KC, 0:NC * B * T].rearrange("p (c b t) -> p c b t", c=NC, b=B),
                                ACT.Copy, scale=hmask[:, 0, j, 0:1])
                    elif name == "G1":
                        ins = g_out(act, copy, src, 1)
                    elif name == "CA1":
                        ins = ca_rows_out(copy, src, 1)
                    else:
                        ins = copy(vw[:, int(name[2]), :], src[:, 0:HID])
                    ins.then_inc(a_drained, 1)
                if step == 0:
                    act.wait_ge(loaded_wout, 32)
                    high(wout_r, wout, 3)

            def front(at, name):
                par = 0 if at == "prologue" else 1 - at.par
                src = piece(at, name)
                if name == "xT01":
                    ins = copy(xT[:, 0:2, :], src[0:KC, :].rearrange("p (c n) -> p c n", c=2))
                elif name == "xT2":
                    ins = copy(xT[:, 2, :], src[0:KC, 0:2 * S])
                elif name == "MT":
                    ins = copy(m[:, :].rearrange("k (b n) -> k b n", b=2),
                               src[:, 0:2 * KL].rearrange("k (b n) -> k b n", b=2)[:, :, 0:HT])
                elif name == "QT01":
                    ins = copy(qT[:, par, 0:2, :], src[0:KC, :].rearrange("p (c n) -> p c n", c=2),
                               SCALE)
                elif name == "QM":
                    ins = copy(qT[0:KL, par, 2, :], src[0:KL, 0:2 * S], SCALE)
                else:
                    ins = copy(v_sb[0:KEYS, par, int(name[1]), :], src[0:KEYS, 0:HID])
                ins.then_inc(a_drained, 1)

            def turn_out(at, name, dst):
                src = piece(at, name)
                copy(dst, src[0:KC, 0:NC * S].rearrange("p (c n) -> p c n", c=NC)) \
                    .then_inc(a_drained, 1)

            def exps(n, par, keys):
                for half in range(2):
                    act.wait_ge(maxed, n * 2 + (half + 1))
                    for h in range(4 * half, 4 * half + 4):
                        k = h % 4
                        last = nc.scalar.activation(
                            probs[:, h, 0:keys], scores[half][:, k * keys:(k + 1) * keys], ACT.Exp,
                            bias=neg_max[:, h:h + 1], accum_out=sums[:, par, h:h + 1])
                    last.then_inc(exped, 1)

            front("prologue", "xT01")
            front("prologue", "xT2")
            act.wait_ge(loaded_wkv, 48)
            high(wk_r, wk, 0)
            act.wait_ge(wca_copied, 1)
            high(wq_r, wq, 1)
            high(wv_r, wv, 2)
            for name in ("QM", "MT", "QT01", "V0", "V1"):
                front("prologue", name)
            exps(0, 0, S)

            def end_work(at):
                src = piece(at, "P3T")
                copy(probs3T[:, :, :], src[:, 0:2 * S].rearrange("p (b n) -> p b n", b=2)) \
                    .then_inc(a_drained, 1)
                turn_out(at, "hsT0", hsT[:, 0])

            def body(at):
                more, first = at.kind != "last", at.kind == "first"
                if not first:
                    end_work(at)
                exps(unit(at, 1), 1, S)
                if not first:
                    turn_out(at, "hsT1", hsT[:, 1])
                if more:
                    front(at, "xT01")
                    front(at, "xT2")
                if first:
                    late(at, 0)
                    late(at, 1)
                exps(unit(at, 2), 0, KEYS)
                if more:
                    front(at, "QM")
                    front(at, "MT")
                turn_out(at, "hs1T0", hs1T[:, 0])
                turn_out(at, "hs1T1", hs1T[:, 1])
                exps(unit(at, 3), 1, KEYS)
                if first:
                    late(at, 2)
                if more:
                    front(at, "QT01")
                    exps(unit(at, 4), 0, S)
                act.wait_ge(d_drained, RING_D.no(at, "sc3")[0] + 1)
                nc.scalar.activation(exp3[:], less3[:], ACT.Exp).then_inc(exp3_made, 1)
                if first:
                    late(at, 3)
                if more:
                    front(at, "V0")
                    front(at, "V1")

            pairs(act, body)
            end_work("epilogue")
            turn_out("epilogue", "hsT1", hsT[:, 1])

        @block.vector
        def _(dve):
            v = nc.vector

            def copy(dst, src):
                return v.tensor_copy(dst, src)

            def piece(at, name):
                n, bank = RING_D.no(at, name)
                dve.wait_ge(d_filled, n + 1)
                return bank_d[bank]

            dve.wait_ge(loaded_ca, 16)
            v.tensor_copy(ca_sel[:, :].rearrange("r (n two) -> r n two", two=2),
                          ca_all[:, :].rearrange("r (n three) -> r n three", three=3)[:, :, 0:2]) \
                .then_inc(ca_picked, 1)
            dve.wait_ge(ca_picked, 1)
            v.tensor_copy(ca_sel[:, S - 1:S], ca_all[:, CAD - 1:CAD]).then_inc(ca_picked, 1)
            v.memset(ca_rows[:].bitcast(U32), 0).then_inc(ca_zeroed, 1)
            v.memset(ca_stack[:, :, :, T * len(CA_PART):], 0.0).then_inc(ca_zeroed, 1)
            dve.wait_ge(made, 5)
            dve.wait_ge(loaded_wq, 64)
            dve.wait_ge(a_drained, RING_A.no("prologue", "WcaT")[0] + 1)
            v.tensor_tensor(wq[:, :, QC:QC + HT].rearrange("p c (h t) -> p c h t", h=HEADS),
                            wca_t[:].unsqueeze(2).broadcast_to([KC, NC, HEADS, T]),
                            hmask[:], ALU.mult).then_inc(wca_copied, 1)

            def low(dst, src, n):
                dve.wait_ge(w_high, n + 1)
                v.tensor_tensor(dst[1][:], src[:], dst[0][:], ALU.subtract).then_inc(w_low, 1)

            def stack_ca():
                def steps_done(n):
                    dve.wait_ge(ca_split, n)
                v.tensor_copy(ca_parts[:, 0, :], caQ[:, :]).then_inc(ca_split, 1)
                steps_done(1)
                v.tensor_tensor(ca_rest[:, :], caQ[:, :], ca_parts[:, 0, :], ALU.subtract) \
                    .then_inc(ca_split, 1)
                steps_done(2)
                v.tensor_copy(ca_parts[:, 1, :], ca_rest[:, :]).then_inc(ca_split, 1)
                steps_done(3)
                for slot, part in enumerate(CA_PART):
                    dst = ca_stack[:, :, :, T * slot:T * slot + T]
                    wide = [t.rearrange("q (b t) -> q b t", t=T).unsqueeze(2)
                            .broadcast_to([S, B, 4, T])
                            for t in (ca_parts[:, 0, :], ca_parts[:, 1, :], ca_rest[:, :])]
                    if part == 2:
                        v.tensor_tensor(dst, wide[2], wide[1], ALU.subtract).then_inc(ca_split, 1)
                    else:
                        v.tensor_copy(dst, wide[part]).then_inc(ca_split, 1)

            def late(at, step):
                for name in LATE_D[step]:
                    src = piece(at, name)
                    if name == "caT":
                        ins = copy(caT[:, :, :], src[0:CC, 0:2 * B * T]
                                   .rearrange("p (c n) -> p c n", c=2))
                    elif name == "WqT1":
                        ins = copy(wqT[:, 1, :], src[0:KC, 0:PAD])
                    elif name == "v2T":
                        for c in range(NC):
                            ins = v.tensor_tensor(
                                v2_blocks[:, c].rearrange("p b (h t) -> p b h t", h=HEADS),
                                src[0:KC, c * B * T:(c + 1) * B * T]
                                    .rearrange("p (b t) -> p b t", b=B)
                                    .unsqueeze(2).broadcast_to([KC, B, HEADS, T]),
                                hmask[:, c].unsqueeze(1).broadcast_to([KC, B, HEADS, T]), ALU.mult)
                    elif name[0] == "G":
                        ins = g_out(dve, lambda o, i, s: v.tensor_scalar(o, i, s, None, ALU.mult),
                                    src, int(name[1]))
                    else:
                        ins = copy(vw[:, int(name[2]), :], src[:, 0:HID])
                    ins.then_inc(d_drained, 1)
                if step == 0:
                    low(wout_r, wout, 3)

            def front(at, name):
                par = 0 if at == "prologue" else 1 - at.par
                src = piece(at, name)
                if name == "ctxT":
                    ins = copy(ctxT[:, :, :], src[0:CC, :].rearrange("p (c n) -> p c n", c=2))
                elif name == "KT01":
                    for j in range(3):
                        for c in range(2):
                            ins = v.tensor_scalar(
                                k_blocks[:, par, c, j],
                                src[0:KC, c * 2 * KEYS:(c + 1) * 2 * KEYS]
                                    .rearrange("p (b k) -> p b k", b=2),
                                hmask[:, 0, j, 0:1], None, ALU.mult)
                elif name == "KT2":
                    for j in range(2):
                        ins = v.tensor_scalar(
                            k_blocks[0:KL, par, 2, j],
                            src[0:KL, 0:2 * KEYS].rearrange("p (b k) -> p b k", b=2),
                            last_mask[:, j:j + 1], None, ALU.mult)
                else:
                    ins = copy(m_rows[:, :, :, :],
                               src[:, 0:2 * S].bitcast(BF16)
                                   .rearrange("p (b g n) -> p b g n", b=2, g=2))
                ins.then_inc(d_drained, 1)

            def maxima(n, keys):
                for half in range(2):
                    dve.wait_ge(scored, n * 2 + (half + 1))
                    v.tensor_reduce(neg_max[:, 4 * half:4 * half + 4],
                                    scores[half][:, 0:4 * keys].rearrange("q (h k) -> q h k", h=4),
                                    AX.X, ALU.max, negate=True).then_inc(maxed, 1)

            def turned_copy(n, keys):
                for half in range(2):
                    dve.wait_ge(turned_full, n * 2 + (half + 1))
                    copy(probsT[0:keys, 4 * half:4 * half + 4, :],
                         turned[half][0:keys, :].rearrange("k (h q) -> k h q", h=4)) \
                        .then_inc(turned_out, 1)

            def norm(at, k):
                n = unit(at, k)
                dve.wait_ge(exped, n * 2 + 2)
                v.reciprocal(recip[:, k % 2, :], sums[:, k % 2, :]).then_inc(inverted, 1)
                src = piece(at, f"PV{k}")
                dve.wait_ge(inverted, n + 1)
                v.tensor_tensor(hs[:, k, 0:HID].rearrange("q (h d) -> q h d", h=HEADS),
                                src[:, 0:HID].rearrange("q (h d) -> q h d", h=HEADS),
                                recip[:, k % 2, :].unsqueeze(2).broadcast_to([S, HEADS, D]),
                                ALU.mult).then_inc(d_drained, 1)

            def split_hidden(at, b):
                base = 4 * (PAIRS - 1) if at == "epilogue" else at.lin(4, -4)
                dve.wait_ge(a_drained, RING_A.no(at, f"hsT{b}")[0] + 1)
                copy(hsT_r[0][:, b], hsT[:, b]).then_inc(hs_split, 1)
                dve.wait_ge(hs_split, base + (2 * b + 1))
                v.tensor_tensor(hsT_r[1][:, b], hsT[:, b], hsT_r[0][:, b], ALU.subtract) \
                    .then_inc(hs_split, 1)

            def finish(at, b, par):
                src = piece(at, f"out{b}")
                if at == "epilogue":
                    dve.wait_ge(xb_made, B)
                    dve.wait_ge(out_free[b], 16 * PAIRS)
                else:
                    dve.wait_ge(xb_made, at.lin(2))
                    dve.wait_ge(out_free[b], at.lin(16))
                v.tensor_tensor(out_sb[:, b, :], src[:, 0:HID], xb[:, par, b, :], ALU.add) \
                    .then_inc(d_drained, 1)

            front("prologue", "ctxT")
            low(wk_r, wk, 0)
            low(wq_r, wq, 1)
            dve.wait_ge(a_drained, RING_A.no("prologue", "caQ")[0] + 1)
            dve.wait_ge(ca_zeroed, 2)
            stack_ca()
            front("prologue", "KT2")
            low(wv_r, wv, 2)
            front("prologue", "KT01")
            src = piece("prologue", "CA0")
            ca_rows_out(copy, src, 0).then_inc(d_drained, 1)
            front("prologue", "MsT")
            maxima(0, S)

            def body(at):
                more, first = at.kind != "last", at.kind == "first"
                turned_copy(unit(at, 0), S)
                maxima(unit(at, 1), S)
                if more:
                    front(at, "ctxT")
                if first:
                    late(at, 0)
                else:
                    split_hidden(at, 0)
                norm(at, 0)
                if not first:
                    finish(at, 0, 1 - at.par)
                    split_hidden(at, 1)
                turned_copy(unit(at, 1), S)
                maxima(unit(at, 2), KEYS)
                if first:
                    late(at, 1)
                if more:
                    front(at, "KT2")
                if not first:
                    finish(at, 1, 1 - at.par)
                norm(at, 1)
                turned_copy(unit(at, 2), KEYS)
                maxima(unit(at, 3), KEYS)
                if more:
                    front(at, "KT01")
                if first:
                    late(at, 2)
                if more:
                    front(at, "MsT")
                norm(at, 2)
                turned_copy(unit(at, 3), KEYS)
                if more:
                    maxima(unit(at, 4), S)
                if first:
                    late(at, 3)
                src = piece(at, "sc3")[:, 0:2 * HT].rearrange("q (h t) -> q h t", t=T)
                v.tensor_reduce(max3[:], src, AX.X, ALU.max).then_inc(max3_made, 1)
                dve.wait_ge(max3_made, at.lin(1, 1))
                v.tensor_tensor(less3[:], src,
                                max3[:].unsqueeze(2).broadcast_to([S, 2 * HEADS, T]),
                                ALU.subtract).then_inc(d_drained, 1)
                dve.wait_ge(exp3_made, at.lin(1, 1))
                v.tensor_reduce(sum3[:, 0, :], exp3[:], AX.X, ALU.add).then_inc(sum3_made, 1)
                dve.wait_ge(sum3_made, at.lin(1, 1))
                v.reciprocal(sum3[:, 1, :], sum3[:, 0, :]).then_inc(inv3_made, 1)
                dve.wait_ge(inv3_made, at.lin(1, 1))
                for b in range(2):
                    v.tensor_tensor(
                        probs3[:, at.par, b, 2 * at.par + b].rearrange("q (h t) -> q h t", t=T),
                        exp3[:, HEADS * b:HEADS * (b + 1)],
                        sum3[:, 1, HEADS * b:HEADS * (b + 1)].unsqueeze(2)
                            .broadcast_to([S, HEADS, T]),
                        ALU.mult).then_inc(probs3_made, 1)
                norm(at, 3)

            pairs(dve, body)
            split_hidden("epilogue", 0)
            split_hidden("epilogue", 1)
            for b in range(2):
                finish("epilogue", b, (PAIRS - 1) % 2)

        @block.tensor
        def _(pe):
            mm = nc.tensor.matmul

            def fill_a(at, name):
                n, bank = RING_A.no(at, name)
                if not (isinstance(n, int) and n < 2):
                    pe.wait_ge(a_drained, n - 1)
                return bank_a[bank]

            def fill_d(at, name):
                n, bank = RING_D.no(at, name)
                if not (isinstance(n, int) and n < 2):
                    pe.wait_ge(d_drained, n - 1)
                return bank_d[bank]

            def got_a(at, name):
                pe.wait_ge(a_drained, RING_A.no(at, name)[0] + 1)

            def got_d(at, name):
                pe.wait_ge(d_drained, RING_D.no(at, name)[0] + 1)

            def turn(dst, src, rows, eye=None):
                return nc.tensor.transpose(dst, src, (ident if eye is None else eye)[0:rows, 0:rows])

            def three(dst, stationary, moving, first=True, last=True):
                for i, (a, b) in enumerate(((0, 0), (0, 1), (1, 0))):
                    ins = mm(dst, stationary(a), moving(b), start=first and i == 0,
                             stop=last and i == 2)
                return ins

            def late(at, step):
                for name in sorted(LATE_A[step] + LATE_D[step], key=LATE_ORDER.index):
                    a = name in LATE_A[step]
                    dst = (fill_a if a else fill_d)(at, name)
                    if name == "caT":
                        for c in range(2):
                            last = turn(dst[0:CC, c * B * T:(c + 1) * B * T],
                                        ca_all[:, c * CC:(c + 1) * CC], B * T)
                    elif name[:3] == "WqT":
                        c = int(name[3])
                        n, col = (KC, c * KC) if c < 2 else (HID - 2 * KC, QC + HT)
                        for r in range(NC):
                            last = turn(dst[0:n, r * KC:(r + 1) * KC], wq[:, r, col:col + n], KC)
                    elif name in ("k2T", "v2T"):
                        pe.wait_ge(loaded_wca, 32)
                        got_d(at, "caT")
                        w = wk_ca if name == "k2T" else wv_ca
                        for c in range(NC):
                            for r in range(2):
                                last = mm(dst[0:KC, c * B * T:(c + 1) * B * T],
                                          w[:, r, c * KC:(c + 1) * KC], caT[:, r, :],
                                          start=r == 0, stop=r == 1)
                    elif name[0] == "G":
                        got_a(at, "WqT2")
                        got_d(at, "WqT1")
                        r = int(name[1])
                        for c in range(NC):
                            rows, heads = (KC, 3) if c < 2 else (HID - 2 * KC, 2)
                            width = B * heads * T
                            last = mm(dst[0:KC, c * B * 3 * T:c * B * 3 * T + width],
                                      wqT[0:rows, c, r * KC:(r + 1) * KC],
                                      k2_blocks[0:rows, c, :, 0:heads * T], start=True, stop=True)
                    elif name[:2] == "VW":
                        pe.wait_ge(loaded_wout, 32)
                        got_d(at, "v2T")
                        n = int(name[2])
                        for c in range(NC):
                            last = mm(dst[:, 0:HID],
                                      v2_blocks[:, c, 4 * n:4 * n + 4, :].rearrange("p b n -> p (b n)"),
                                      wout[:, c, :], start=c == 0, stop=c == NC - 1)
                    else:
                        last = turn_ca(dst, 1)
                    last.then_inc(a_filled if a else d_filled, 1)

            def turn_ca(dst, n):
                for b in range(8):
                    last = turn(dst.bitcast(BF16)[:, b * S:(b + 1) * S],
                                ca_stack[:, 8 * n + b].rearrange("q j n -> q (j n)"), S, ident16)
                return last

            def front(at, name):
                par = 0 if at == "prologue" else 1 - at.par
                seen = 16 if at == "prologue" else at.next().half(16, 16)
                split = (lambda per: per) if at == "prologue" else (lambda per: at.lin(per, 2 * per))
                a = name in RING_A.lists["prologue"]
                dst = (fill_a if a else fill_d)(at, name)
                if name in ("xT01", "xT2"):
                    if name == "xT01":
                        pe.wait_ge(loaded_x[par], seen)
                    for i, c in enumerate((0, 1) if name == "xT01" else (2,)):
                        for b in range(2):
                            last = turn(dst[0:KC, (2 * i + b) * S:(2 * i + b + 1) * S],
                                        x_sb[:, par, b, c * KC:(c + 1) * KC], S)
                elif name == "ctxT":
                    pe.wait_ge(loaded_ctx[par], seen)
                    for c in range(2):
                        for b in range(2):
                            last = turn(dst[0:CC, (2 * c + b) * S:(2 * c + b + 1) * S],
                                        ctx_sb[:, par, b, c * CC:(c + 1) * CC], S)
                elif name in ("QM", "QT01"):
                    if name == "QM":
                        pe.wait_ge(x_split, split(4))
                    for i, c in enumerate((2,) if name == "QM" else (0, 1)):
                        rows = KL if c == 2 else KC
                        for r in range(NC):
                            last = three(dst[0:rows, i * 2 * S:(i + 1) * 2 * S],
                                         lambda k: wq_r[k][:, r, Q_CHUNKS[c]],
                                         lambda k: xT_r[k][:, r, :], r == 0, r == NC - 1)
                elif name == "MT":
                    got_a(at, "QM")
                    for b in range(2):
                        last = turn(dst[:, b * KL:(b + 1) * KL],
                                    qT[0:KL, par, 2, b * S:(b + 1) * S], KL)
                elif name in ("KT01", "KT2"):
                    if name == "KT2":
                        pe.wait_ge(ctx_split, split(2))
                    for i, c in enumerate((0, 1) if name == "KT01" else (2,)):
                        rows = KL if c == 2 else KC
                        for r in range(2):
                            last = three(dst[0:rows, i * 2 * KEYS:(i + 1) * 2 * KEYS],
                                         lambda k: wk_r[k][:, r, Q_CHUNKS[c]],
                                         lambda k: ctxT_r[k][:, r, :]
                                         .rearrange("p (b k) -> p b k", b=2)[:, :, 0:KEYS],
                                         r == 0, r == 1)
                elif name in ("V0", "V1"):
                    b = int(name[1])
                    for r in range(2):
                        last = three(dst[0:KEYS, 0:HID],
                                     lambda k: ctxT_r[k][:, r, b * S:b * S + KEYS],
                                     lambda k: wv_r[k][:, r, :], r == 0, r == 1)
                else:
                    pe.wait_ge(m_step, split(9))
                    dst = dst.bitcast(BF16)
                    for b in range(2):
                        for k in range(2):
                            last = turn(dst[:, (2 * b + k) * S:(2 * b + k + 1) * S],
                                        m_stack[:, b, 4 * k:4 * k + 4, :]
                                            .rearrange("q h n -> q (h n)"), S, ident16)
                last.then_inc(a_filled if a else d_filled, 1)

            def channel_scores(n, at, b):
                row = at.lin(2, b)
                for half in range(2):
                    for k in range(4):
                        last = mm(scores[half][:, k * S:(k + 1) * S],
                                  ca_rows[:, bass.ds(row, 1), k, :].rearrange("p b q -> p (b q)"),
                                  m_rows[:, b, half, :], start=True, stop=True)
                    last.then_inc(scored, 1)

            def token_scores(at, b):
                tok = slice(b * S, (b + 1) * S)
                for half, runs in enumerate((((0, 0, 3), (1, 0, 1)), ((1, 1, 2), (2, 0, 2)))):
                    col = 0
                    for c, j, heads in runs:
                        width, rows = heads * KEYS, KL if c == 2 else KC
                        last = mm(scores[half][:, col:col + width], qT[0:rows, at.par, c, tok],
                                  k_blocks[0:rows, at.par, c, j:j + heads, b, :],
                                  start=True, stop=True)
                        col += width
                    last.then_inc(scored, 1)

            def turn_probs(n, keys):
                for half in range(2):
                    pe.wait_ge(exped, n * 2 + (half + 1))
                    for k in range(4):
                        last = turn(turned[half][0:keys, k * S:(k + 1) * S],
                                    probs[:, 4 * half + k, 0:keys], S)
                    last.then_inc(turned_full, 1)

            def weigh(at, k):
                n, b, keys = unit(at, k), k % 2, S if k < 2 else KEYS
                values = x_sb if k < 2 else v_sb
                dst = fill_d(at, f"PV{k}")
                pe.wait_ge(turned_out, n * 2 + 2)
                for h in range(HEADS):
                    last = mm(dst[:, h * D:(h + 1) * D], probsT[0:keys, h, :],
                              values[0:keys, at.par, b, h * D:(h + 1) * D], start=True, stop=True)
                last.then_inc(d_filled, 1)

            def turn_hidden(at, name, k, after):
                dst = fill_a(at, name)
                pe.wait_ge(d_drained, after + 1)
                for c in range(NC):
                    last = turn(dst[0:KC, c * S:(c + 1) * S], hs[:, k, c * KC:(c + 1) * KC], S)
                last.then_inc(a_filled, 1)

            def turn_probs3(at, par):
                dst = fill_a(at, "P3T")
                pe.wait_ge(probs3_made, 2 * PAIRS if at == "epilogue" else at.lin(2))
                for b in range(2):
                    last = turn(dst[:, b * S:(b + 1) * S],
                                probs3[:, par, b].rearrange("q j n -> q (j n)"), S)
                last.then_inc(a_filled, 1)

            def project(at, b, group):
                dst = fill_d(at, f"out{b}")
                got_a(at, "P3T")
                mm(dst[:, 0:HID], probs3T[:, b, :],
                   vw[:, bass.ds(group, 1), :].rearrange("p g n -> p (g n)"),
                   start=True, stop=False)
                base = 4 * (PAIRS - 1) if at == "epilogue" else at.lin(4, -4)
                pe.wait_ge(hs_split, base + (2 * b + 2))
                for c in range(NC):
                    last = three(dst[:, 0:HID], lambda k: hsT_r[k][:, b, c, :],
                                 lambda k: wout_r[k][:, c, :], False, c == NC - 1)
                last.then_inc(d_filled, 1)

            pe.wait_ge(made, 2)
            pe.wait_ge(zeroed, 5)
            front("prologue", "ctxT")
            pe.wait_ge(loaded_ca, 16)
            pe.wait_ge(ca_picked, 2)
            dst = fill_a("prologue", "caQ")
            turn(dst[:, 0:B * T], ca_sel[:, :], B * T).then_inc(a_filled, 1)
            pe.wait_ge(loaded_wqca, 16)
            dst = fill_a("prologue", "WcaT")
            for c in range(NC):
                last = turn(dst[0:KC, c * T:(c + 1) * T], wq_ca[:, c * KC:(c + 1) * KC], T)
            last.then_inc(a_filled, 1)
            front("prologue", "xT01")
            front("prologue", "xT2")
            pe.wait_ge(w_low, 1)
            front("prologue", "KT2")
            pe.wait_ge(w_low, 2)
            front("prologue", "QM")
            front("prologue", "KT01")
            front("prologue", "MT")
            front("prologue", "QT01")
            pe.wait_ge(ca_split, 3 + len(CA_PART))
            pe.wait_ge(made, 11)
            dst = fill_d("prologue", "CA0")
            turn_ca(dst, 0).then_inc(d_filled, 1)
            pe.wait_ge(w_low, 3)
            front("prologue", "V0")
            front("prologue", "V1")
            front("prologue", "MsT")
            got_d("prologue", "MsT")
            channel_scores(0, At(0, 0, 0, "first"), 0)

            def body(at):
                more, first = at.kind != "last", at.kind == "first"
                group = at.half(1) if at.par else at.half(1, -1)
                turn_probs(unit(at, 0), S)
                channel_scores(unit(at, 1), at, 1)
                if more:
                    front(at, "ctxT")
                if not first:
                    prev = RING_D.no(at, of_d(0, 1, more)[0])[0] - 1
                    turn_probs3(at, 1 - at.par)
                    turn_hidden(at, "hsT0", 2, prev)
                if first:
                    front(at, "xT01")
                    front(at, "xT2")
                    pe.wait_ge(made, 15)
                    late(at, 0)
                weigh(at, 0)
                if not first:
                    turn_hidden(at, "hsT1", 3, prev)
                    if more:
                        front(at, "xT01")
                    project(at, 0, group)
                    if more:
                        front(at, "xT2")
                turn_probs(unit(at, 1), S)
                token_scores(at, 0)
                if first:
                    late(at, 1)
                    pe.wait_ge(w_low, 4)
                if more:
                    front(at, "KT2")
                if not first:
                    project(at, 1, group)
                weigh(at, 1)
                if more:
                    front(at, "QM")
                turn_probs(unit(at, 2), KEYS)
                token_scores(at, 1)
                if more:
                    front(at, "MT")
                turn_hidden(at, "hs1T0", 0, RING_D.no(at, "PV0")[0])
                if more:
                    front(at, "KT01")
                turn_hidden(at, "hs1T1", 1, RING_D.no(at, "PV1")[0])
                if first:
                    late(at, 2)
                if more:
                    front(at, "QT01")
                    front(at, "MsT")
                weigh(at, 2)
                turn_probs(unit(at, 3), KEYS)
                if more:
                    got_d(at, "MsT")
                    channel_scores(unit(at, 4), at.next(), 0)
                if first:
                    late(at, 3)
                dst = fill_d(at, "sc3")
                got_a(at, "hs1T1")
                for b in range(2):
                    for c in range(NC):
                        last = mm(dst[:, b * HT:(b + 1) * HT], hs1T[:, b, c, :],
                                  g[:, c, bass.ds(at.lin(2, b), 1), :].rearrange("p b n -> p (b n)"),
                                  start=c == 0, stop=c == NC - 1)
                last.then_inc(d_filled, 1)
                if more:
                    front(at, "V0")
                    front(at, "V1")
                weigh(at, 3)

            pairs(pe, body)
            turn_probs3("epilogue", (PAIRS - 1) % 2)
            turn_hidden("epilogue", "hsT0", 2, RING_D.no("epilogue", "out0")[0] - 1)
            turn_hidden("epilogue", "hsT1", 3, RING_D.no("epilogue", "out0")[0] - 1)
            for b in range(2):
                project("epilogue", b, (PAIRS - 1) // 2)


_INS = ['x', 'ctx_768', 'L0_xattn_Wq', 'L0_xattn_Wk', 'L0_xattn_Wv', 'L0_xattn_Wq_ca', 'L0_xattn_Wk_ca',
        'L0_xattn_Wv_ca', 'L0_xattn_Wout', 'L0_xattn_b_out']


def kernel(**inputs):
    import numpy as np
    import concourse.bacc as bacc
    from concourse import mybir as mb
    from concourse.bass_utils import run_bass_kernel_spmd

    nc = bacc.Bacc("TRN2", target_bir_lowering=False, num_devices=1)
    arrays, args = {}, []
    for name in _INS:
        a = np.ascontiguousarray(inputs[name])
        arrays[f"in_{name}"] = a
        args.append(nc.dram_tensor(f"in_{name}", a.shape, mb.dt.from_np(a.dtype), kind="ExternalInput").ap())
    args.append(nc.dram_tensor("out_0", (B, S, HID), mb.dt.float32, kind="ExternalOutput").ap())
    attention(nc, *args)
    r = run_bass_kernel_spmd(nc, [arrays], core_ids=[0])
    return r.results[0]["out_0"]
```

```python
from contextlib import ExitStack

import concourse.bass as bass
from concourse import mybir

F32 = mybir.dt.float32
F32R = mybir.dt.float32r
BF16 = mybir.dt.bfloat16
U32 = mybir.dt.uint32
ACT = mybir.ActivationFunctionType
ALU = mybir.AluOpType
AX = mybir.AxisListType

B, S, HID = 16, 128, 320
CAD, T = 192, 4
HEADS = 8
D = HID // HEADS
SCALE = float(D) ** -0.5
KEYS = S - T
PAIRS = B // 2
KC = 3 * D
NC = 3
PAD = KC * NC
CC = CAD // 2
HT = HEADS * T
QC = 2 * KC
QW = HID + HT
Q_CHUNKS = [slice(0, KC), slice(KC, QC), slice(QC, QW)]
KL = QW - QC
M_PART = [0, 0, 0, 1, 1, 2]
CA_PART = [0, 1, 2, 0, 1, 0]
MAX_COL = T * len(M_PART)
VW_PART = [0, 1, 0, 1]


class At:

    def __init__(self, j, a, b, kind):
        self.j, self.a, self.b, self.kind = j, a, b, kind
        self.par = b % 2

    def lin(self, per, off=0):
        if self.a == 0:
            return per * self.b + off
        return self.j * (per * self.a) + (per * self.b + off)

    def half(self, per, off=0):
        if self.a == 0:
            return per * (self.b // 2) + off
        return self.j * per + (per * (self.b // 2) + off)

    def next(self):
        return At(self.j, self.a, self.b + 1, "next")


class Ring:

    def __init__(self, prologue, first, mid, last, epilogue):
        self.lists = dict(prologue=prologue, first=first, mid=mid, last=last, epilogue=epilogue)

    def no(self, at, name):
        n = {k: len(v) for k, v in self.lists.items()}
        if at == "prologue":
            k = self.lists["prologue"].index(name)
            return k, k % 2
        if at == "epilogue":
            k = n["prologue"] + n["first"] + (PAIRS - 2) * n["mid"] + n["last"]
            k += self.lists["epilogue"].index(name)
            return k, k % 2
        k = self.lists[at.kind].index(name)
        if at.kind == "first":
            k += n["prologue"]
            return k, k % 2
        k += n["prologue"] + n["first"] - n["mid"]
        return at.lin(n["mid"], k), (n["mid"] * at.b + k) % 2


LATE_D = [["v2T"], ["VW0", "VW1"], ["VW2", "VW3"], ["CA1"]]


def of_a(end, front):
    return (end * ["P3T"] + front * ["ctxT"] + end * ["hsT0", "hsT1"]
            + front * ["xT01", "xT2", "QM", "MT", "XG", "QT01", "V0", "V1"])


def of_d(late, end, front):
    return (["PV0"] + late * LATE_D[0] + end * ["out0"]
            + front * ["KT2"] + late * LATE_D[1] + end * ["out1"] + ["PV1"]
            + front * ["KT01"] + late * LATE_D[2] + front * ["MsT"] + ["PV2"]
            + late * LATE_D[3] + ["PV3"])


RING_A = Ring(["xT01", "xT2", "WcaT", "caQ", "caT", "WqT0", "WqT1", "QM", "WqT2", "MT", "ctxT",
               "k2T", "QT01", "G0", "V0", "G2", "V1", "XG"],
              of_a(0, 1), of_a(1, 1), of_a(1, 0), ["hsT0", "hsT1", "P3T"])
RING_D = Ring(["CA0", "MsT", "G1", "KT2", "KT01"],
              of_d(1, 0, 1), of_d(0, 1, 1), of_d(0, 1, 0), ["out0", "out1"])


def attention(nc, x, ctx, Wq, Wk, Wv, Wq_ca, Wk_ca, Wv_ca, Wout, b_out, out):
    with ExitStack() as stack:
        def sb(name, shape, dt=F32):
            return stack.enter_context(nc.sbuf_tensor(name, shape, dt))

        def ps(name, dt=F32):
            return stack.enter_context(nc.psum_tensor(name, [128, 512], dt))

        def sem(name):
            return stack.enter_context(nc.semaphore(name))

        wq = sb("wq", [KC, NC, QW])
        wk = sb("wk", [CC, 2, QW])
        wv = sb("wv", [CC, 2, HID])
        wk_ca = sb("wk_ca", [CC, 2, PAD])
        wv_ca = sb("wv_ca", [CC, 2, PAD])
        wout = sb("wout", [KC, NC, HID])
        wq_ca = sb("wq_ca", [T, PAD])
        wq_r = [sb(f"wq_r{i}", [KC, NC, QW], F32R) for i in range(2)]
        wk_r = [sb(f"wk_r{i}", [CC, 2, QW], F32R) for i in range(2)]
        wv_r = [sb(f"wv_r{i}", [CC, 2, HID], F32R) for i in range(2)]
        wout_r = [sb(f"wout_r{i}", [KC, NC, HID], F32R) for i in range(2)]
        bias = sb("bias", [128, HID])
        ident = sb("ident", [128, 128])
        ident16 = sb("ident16", [128, 128], BF16)
        zeros = sb("zeros", [128, 2 * 2 * S])
        hmask = sb("hmask", [KC, NC, HEADS, T])
        ca_all = sb("ca_all", [B * T, CAD])
        ca_sel = sb("ca_sel", [B * T, S])
        caT = sb("caT", [CC, 2, B * T])
        caQ = sb("caQ", [S, B * T])
        ca_rest = sb("ca_rest", [S, B * T])
        ca_parts = sb("ca_parts", [S, 2, B * T], BF16)
        ca_stack = sb("ca_stack", [S, B, 4, 32], BF16)
        ca_rows = sb("ca_rows", [128, B, S], BF16)
        ca_now = sb("ca_now", [128, 2, 4, S], BF16)
        ca_less = sb("ca_less", [128, 4, S], BF16)
        wca_t = sb("wca_t", [KC, NC, T])
        wqT = sb("wqT", [KC, NC, PAD])
        k2_blocks = sb("k2_blocks", [KC, NC, B, 3 * T])
        v2_blocks = sb("v2_blocks", [KC, NC, B, HT])
        g_blocks = sb("g_blocks", [KC, NC, B, 3, HT])
        vw_parts = [sb(f"vw_part{i}", [128, B // 4, HID], F32R) for i in range(2)]
        vw_stack = sb("vw_stack", [128, B, HID], F32R)
        x_sb = sb("x_sb", [S, 2, 2, PAD])
        ctx_sb = sb("ctx_sb", [S, 2, 2, CAD])
        xb = sb("xb", [S, 2, 2, HID])
        xT = sb("xT", [KC, NC, 2 * S])
        ctxT = sb("ctxT", [CC, 2, 2 * S])
        xT_r = [sb(f"xT_r{i}", [KC, NC, 2 * S], F32R) for i in range(2)]
        ctxT_r = [sb(f"ctxT_r{i}", [CC, 2, 2 * S], F32R) for i in range(2)]
        qT = sb("qT", [KC, 2, NC, 2 * S])
        k_blocks = sb("k_blocks", [KC, 2, 3, 2, KEYS])
        k_last = sb("k_last", [KL, 2, 2, 2, KEYS])
        v_sb = sb("v_sb", [S, 2, 2, HID])
        m = sb("m", [S, 2 * HT])
        m_rest = sb("m_rest", [S, 2 * HT])
        m_parts = sb("m_parts", [S, 2, 2 * HT], BF16)
        m_stack = sb("m_stack", [S, 2, HEADS, 32], BF16)
        m_rows = sb("m_rows", [128, 2, 2, S], BF16)
        neg_max = sb("neg_max", [S, HEADS])
        max_rest = sb("max_rest", [S, HEADS])
        probs = sb("probs", [S, HEADS, S])
        sums = sb("sums", [S, 2, HEADS])
        recip = sb("recip", [S, 2, HEADS])
        probsT = sb("probsT", [S, HEADS, S])
        hs = sb("hs", [S, 2, PAD])
        xg = sb("xg", [S, 2, HEADS, HT + 1])
        hsT = sb("hsT", [KC, 2, NC, S])
        hsT_r = [sb(f"hsT_r{i}", [KC, 2, NC, S], F32R) for i in range(2)]
        by_head = sb("by_head", [S, 2, HEADS, HT])
        scores3 = sb("scores3", [S, 2, HT])
        max3 = sb("max3", [S, 2 * HEADS])
        less3 = sb("less3", [S, 2 * HEADS, T])
        exp3 = sb("exp3", [S, 2 * HEADS, T])
        sum3 = sb("sum3", [S, 2, 2 * HEADS])
        p3 = sb("p3", [S, 2, HT])
        probs3 = sb("probs3", [S, 2, 4, HT], F32R)
        probs3T = sb("probs3T", [128, 2, S], F32R)
        out_sb = sb("out_sb", [S, 2, HID])

        scores = [ps("scores0"), ps("scores1")]
        turned = [ps("turned0"), ps("turned1")]
        bank_a = [ps("bank_a0"), ps("bank_a1")]
        bank_d = [ps("bank_d0"), ps("bank_d1")]

        loaded_wqca = sem("loaded_wqca")
        loaded_ca = sem("loaded_ca")
        loaded_wq = sem("loaded_wq")
        loaded_wca = sem("loaded_wca")
        loaded_wout = sem("loaded_wout")
        loaded_wkv = sem("loaded_wkv")
        loaded_bias = sem("loaded_bias")
        loaded_x = [sem("loaded_x0"), sem("loaded_x1")]
        loaded_ctx = [sem("loaded_ctx0"), sem("loaded_ctx1")]
        out_free = [sem("out_free0"), sem("out_free1")]
        zeroed = sem("zeroed")
        made = sem("made")
        ca_split = sem("ca_split")
        w_parts = sem("w_parts")
        wq_split = sem("wq_split")
        ctx_split = sem("ctx_split")
        x_split = sem("x_split")
        hs_split = sem("hs_split")
        m_step = sem("m_step")
        xb_made = sem("xb_made")
        ca_picked = sem("ca_picked")
        wca_step = sem("wca_step")
        a_filled = sem("a_filled")
        a_drained = sem("a_drained")
        d_filled = sem("d_filled")
        d_drained = sem("d_drained")
        scored = sem("scored")
        maxed = sem("maxed")
        max_split = sem("max_split")
        stack_turned = sem("stack_turned")
        placed = sem("placed")
        exped = sem("exped")
        turned_full = sem("turned_full")
        turned_out = sem("turned_out")
        inverted = sem("inverted")
        scores3_made = sem("scores3_made")
        max3_made = sem("max3_made")
        less3_made = sem("less3_made")
        exp3_made = sem("exp3_made")
        sum3_made = sem("sum3_made")
        inv3_made = sem("inv3_made")
        probs3_made = sem("probs3_made")
        vw_high = sem("vw_high")
        vw_stacked = sem("vw_stacked")

        def g_out(masked, src, r):
            for c in range(NC):
                heads = 3 if c < 2 else 2
                for j in range(3 if r < 2 else 2):
                    last = masked(g_blocks[:, r, :, j, 3 * T * c:3 * T * c + heads * T],
                                  src[0:KC, c * B * 3 * T:c * B * 3 * T + B * heads * T]
                                      .rearrange("p (b n) -> p b n", b=B), hmask[:, 0, j, 0:1])
            return last

        block = stack.enter_context(nc.Block())

        def pairs(engine, body):
            body(At(0, 0, 0, "first"))
            with engine.Fori(0, (PAIRS - 2) // 2) as j:
                body(At(j, 2, 1, "mid"))
                body(At(j, 2, 2, "mid"))
            body(At(0, 0, PAIRS - 1, "last"))

        def unit(at, k):
            return at.lin(4, k)

        @block.sync
        def _(sp):
            def load_x(row, par):
                sp.dma_start(x_sb[:, par, :, 0:HID], x[bass.ds(row, 2)].rearrange("b s h -> s b h")) \
                    .then_inc(loaded_x[par], 16)

            def load_ctx(row, par):
                sp.dma_start(ctx_sb[:, par, :, :], ctx[bass.ds(row, 2)].rearrange("b s h -> s b h")) \
                    .then_inc(loaded_ctx[par], 16)

            def store(b, row):
                sp.dma_start(out[bass.ds(row, 1)].rearrange("b s h -> (b s) h"), out_sb[:, b, :]) \
                    .then_inc(out_free[b], 16)

            load_x(0, 0)
            sp.dma_start(ca_all[:, 0:CAD], ctx[:, KEYS:S, :]).then_inc(loaded_ca, 16)
            load_ctx(0, 0)
            sp.dma_start(wk[:, :, 0:HID], Wk.rearrange("(c p) n -> p c n", p=CC)) \
                .then_inc(loaded_wkv, 16)
            sp.dma_start(wv[:, :, :], Wv.rearrange("(c p) n -> p c n", p=CC)).then_inc(loaded_wkv, 16)
            sp.dma_start(bias[:, :], b_out.partition_broadcast(128)).then_inc(loaded_bias, 16)
            for w2, w2_sb in ((Wk_ca, wk_ca), (Wv_ca, wv_ca)):
                sp.dma_start(w2_sb[:, :, 0:HID], w2.rearrange("(c p) n -> p c n", p=CC)) \
                    .then_inc(loaded_wca, 16)
            load_x(2, 1)
            load_ctx(2, 1)
            sp.wait_ge(zeroed, 4)
            sp.dma_start(wout[:, 0:2, :], Wout[0:2 * KC, :].rearrange("(c p) n -> p c n", p=KC)) \
                .then_inc(loaded_wout, 16)
            sp.dma_start(wout[0:HID - 2 * KC, 2, :], Wout[2 * KC:HID, :]).then_inc(loaded_wout, 16)

            def fixed(value):
                return value if isinstance(value, int) else sp.snap(value)

            def body(at):
                loads = at.kind != "last" and not (at.a == 0 and at.b + 2 >= PAIRS)
                if at.kind != "first":
                    before = [fixed(at.lin(2, b - 2)) for b in range(2)]
                    out_made = [fixed(RING_D.no(at, f"out{b}")[0] + 1) for b in range(2)]
                if loads:
                    ahead = fixed(at.lin(2, 4))
                    x_used = fixed(RING_D.no(at, "PV1")[0] + 1)
                if at.kind != "first":
                    for b in range(2):
                        sp.wait_ge(d_drained, out_made[b])
                        store(b, before[b])
                if loads:
                    sp.wait_ge(d_filled, x_used)
                    load_x(ahead, at.par)
                    load_ctx(ahead, at.par)

            body(At(0, 0, 0, "first"))
            sp.wait_ge(d_drained, RING_D.no(At(0, 0, 0, "first"), "VW3")[0] + 1)
            for slot, part in enumerate(VW_PART):
                for r in range(4):
                    sp.dma_start(
                        vw_stack[HT * slot:HT * slot + HT].bitcast(F32)
                            .rearrange("p (n s) h -> p n s h", s=4)[:, :, r, :],
                        vw_parts[part][HT * r:HT * r + HT].bitcast(F32)).then_inc(vw_stacked, 16)
            with sp.Fori(0, (PAIRS - 2) // 2 - 1) as j:
                body(At(j, 2, 1, "mid"))
                body(At(j, 2, 2, "mid"))
            body(At(0, 0, PAIRS - 3, "mid"))
            body(At(0, 0, PAIRS - 2, "mid"))
            body(At(0, 0, PAIRS - 1, "last"))
            for b in range(2):
                sp.wait_ge(d_drained, RING_D.no("epilogue", f"out{b}")[0] + 1)
                store(b, B - 2 + b)
            for b in range(2):
                sp.wait_ge(out_free[b], 16 * (PAIRS + 1))

        @block.gpsimd
        def _(pool):
            gp = nc.gpsimd
            gp.memset(wq[:, 2, :], 0.0).then_inc(zeroed, 1)
            gp.memset(x_sb[:, :, :, HID:PAD], 0.0).then_inc(zeroed, 1)
            gp.memset(wq_ca[:, HID:PAD], 0.0).then_inc(zeroed, 1)
            gp.memset(ident[:], 0.0).then_inc(made, 1)
            pool.wait_ge(made, 1)
            gp.affine_select(out=ident[:], in_=ident[:], compare_op=ALU.not_equal, fill=1.0, base=0,
                             pattern=[[-1, 128]], channel_multiplier=1).then_inc(made, 1)
            gp.memset(wout[:, 2, :], 0.0).then_inc(zeroed, 1)
            gp.memset(hmask[:], 1.0).then_inc(made, 1)
            pool.wait_ge(made, 3)
            gp.affine_select(out=hmask[:], in_=hmask[:], compare_op=ALU.is_ge, fill=0.0, base=0,
                             pattern=[[KC, NC], [-D, HEADS], [0, T]], channel_multiplier=1) \
                .then_inc(made, 1)
            pool.wait_ge(made, 4)
            gp.affine_select(out=hmask[:], in_=hmask[:], compare_op=ALU.is_ge, fill=0.0, base=D - 1,
                             pattern=[[-KC, NC], [D, HEADS], [0, T]], channel_multiplier=-1) \
                .then_inc(made, 1)
            gp.memset(zeros[:], 0.0).then_inc(made, 1)
            gp.memset(m_stack[:, :, :, MAX_COL:], 0.0).then_inc(made, 1)
            pool.wait_ge(made, 7)
            gp.memset(m_stack[:, :, 0:4, MAX_COL:MAX_COL + 3], 1.0).then_inc(made, 1)
            gp.memset(m_stack[:, :, 4:8, MAX_COL + 3:MAX_COL + 6], 1.0).then_inc(made, 1)
            gp.tensor_copy(ident16[:], ident[:]).then_inc(made, 1)
            gp.memset(wk[:, :, HID:QW], 0.0).then_inc(made, 1)
            for t in (wk_ca[:, :, HID:PAD], wv_ca[:, :, HID:PAD]):
                gp.memset(t, 0.0).then_inc(made, 1)

            def split(src, rest, parts, base, done):
                gp.tensor_tensor(parts[:, 0, :], src, zeros[:, 0:2 * HT], ALU.add).then_inc(done, 1)
                pool.wait_ge(done, base + 1)
                gp.tensor_tensor(rest[:, :], src, parts[:, 0, :], ALU.subtract).then_inc(done, 1)
                pool.wait_ge(done, base + 2)
                gp.tensor_tensor(parts[:, 1, :], rest[:, :], zeros[:, 0:2 * HT], ALU.add) \
                    .then_inc(done, 1)
                pool.wait_ge(done, base + 3)

            def split_r(src, parts, base, done):
                rows, n = src.shape[0], src.shape[1]
                gp.tensor_tensor(parts[0], src, zeros[0:rows, 0:n], ALU.add).then_inc(done, 1)
                pool.wait_ge(done, base + 1)
                gp.tensor_tensor(parts[1], src, parts[0], ALU.subtract).then_inc(done, 1)

            def split_front(at):
                pool.wait_ge(a_drained, RING_A.no(at, "ctxT")[0] + 1)
                split_r(ctxT[:].rearrange("p c n -> p (c n)"),
                        [t[:].rearrange("p c n -> p (c n)") for t in ctxT_r], at.lin(2, 2), ctx_split)
                for i, (piece, c) in enumerate((("xT01", slice(0, 2)), ("xT2", slice(2, 3)))):
                    pool.wait_ge(a_drained, RING_A.no(at, piece)[0] + 1)
                    split_r(xT[:, c].rearrange("p c n -> p (c n)"),
                            [t[:, c].rearrange("p c n -> p (c n)") for t in xT_r],
                            at.lin(4, 4) + 2 * i, x_split)

            def stack_m(at):
                base = at.lin(9, 9)
                pool.wait_ge(a_drained, RING_A.no(at, "MT")[0] + 1)
                split(m[:, :], m_rest, m_parts, base, m_step)
                for slot, part in sorted(enumerate(M_PART), key=lambda sp: -sp[1]):
                    dst = m_stack[:, :, :, T * slot:T * slot + T].rearrange("k b h t -> k (b h) t")
                    src = (m_rest[:, :] if part == 2 else m_parts[:, part, :]) \
                        .rearrange("k (bh t) -> k bh t", t=T)
                    if part == 2:
                        less = m_parts[:, 1, :].rearrange("k (bh t) -> k bh t", t=T)
                        gp.tensor_tensor(dst, src, less, ALU.subtract).then_inc(m_step, 1)
                    else:
                        gp.tensor_copy(dst, src).then_inc(m_step, 1)

            def add_bias(par):
                for b in range(2):
                    gp.tensor_tensor(xb[:, par, b, :], x_sb[:, par, b, 0:HID], bias[:, :],
                                     ALU.add).then_inc(xb_made, 1)

            def split_weight(w, parts, n):
                for c in range(w.shape[1]):
                    cols = w.shape[2]
                    ins = gp.tensor_tensor(parts[0][:, c], w[:, c], zeros[0:w.shape[0], 0:cols],
                                           ALU.add)
                ins.then_inc(w_parts, 1)
                pool.wait_ge(w_parts, 2 * n + 1)
                gp.tensor_tensor(parts[1][:], w[:], parts[0][:], ALU.subtract).then_inc(w_parts, 1)

            pool.wait_ge(loaded_wkv, 32)
            pool.wait_ge(made, 11)
            split_weight(wk, wk_r, 0)
            split_weight(wv, wv_r, 1)
            for b in range(2):
                gp.memset(out_sb[:, b, 0:2], 0.0).then_inc(out_free[b], 16)
            gp.memset(xg[:, :, :, HT:HT + 1], 1.0).then_inc(made, 1)
            gp.memset(hs[:, :, HID:PAD], 0.0).then_inc(made, 1)
            pool.wait_ge(loaded_wout, 32)
            split_weight(wout, wout_r, 2)
            pool.wait_ge(loaded_bias, 16)
            pool.wait_ge(loaded_x[0], 16)
            add_bias(0)

            def body(at):
                if at.kind == "last":
                    return
                split_front(at)
                if at.kind != "first":
                    pool.wait_ge(d_drained, RING_D.no(at, "out1")[0] + 1)
                pool.wait_ge(loaded_x[1 - at.par], at.next().half(16, 16))
                add_bias(1 - at.par)
                stack_m(at)

            pairs(pool, body)

        @block.scalar
        def _(act):
            def copy(dst, src, scale=1.0):
                return nc.scalar.activation(dst, src, ACT.Copy, scale=scale)

            def piece(at, name):
                n, bank = RING_A.no(at, name)
                act.wait_ge(a_filled, n + 1)
                return bank_a[bank]

            act.wait_ge(zeroed, 1)
            act.dma_start(wq[:, 0:2, 0:HID], Wq[0:2 * KC, :].rearrange("(c p) n -> p c n", p=KC)) \
                .then_inc(loaded_wq, 16)
            act.dma_start(wq[0:HID - 2 * KC, 2, 0:HID], Wq[2 * KC:HID, :]).then_inc(loaded_wq, 16)
            act.dma_start(wq_ca[:, 0:HID], Wq_ca).then_inc(loaded_wqca, 16)

            def split_x(piece_name, chunks, n):
                src = piece("prologue", piece_name)[0:KC, 0:n * 2 * S].rearrange("p (c n) -> p c n", c=n)
                copy(xT_r[0][:, chunks, :], src).then_inc(x_split, 1)
                copy(xT[:, chunks, :], src).then_inc(a_drained, 1)

            split_x("xT01", slice(0, 2), 2)
            split_x("xT2", slice(2, 3), 1)

            def setup(name):
                src = piece("prologue", name)
                if name == "WcaT":
                    ins = copy(wca_t[:, :, :], src[0:KC, 0:NC * T].rearrange("p (c t) -> p c t", c=NC))
                elif name == "caQ":
                    ins = copy(caQ[:, :], src[:, 0:B * T])
                elif name == "caT":
                    ins = copy(caT[:, :, :], src[0:CC, 0:2 * B * T]
                               .rearrange("p (c n) -> p c n", c=2))
                elif name[:3] == "WqT":
                    c = int(name[3])
                    rows = KC if c < 2 else HID - 2 * KC
                    ins = copy(wqT[0:rows, c, :], src[0:rows, 0:PAD])
                elif name == "k2T":
                    act.wait_ge(made, 5)
                    for j in range(3):
                        ins = nc.scalar.activation(
                            k2_blocks[:, :, :, T * j:T * j + T],
                            src[0:KC, 0:NC * B * T].rearrange("p (c b t) -> p c b t", c=NC, b=B),
                            ACT.Copy, scale=hmask[:, 0, j, 0:1])
                else:
                    ins = g_out(copy, src, int(name[1]))
                ins.then_inc(a_drained, 1)

            def front(at, name):
                par = 0 if at == "prologue" else 1 - at.par
                src = piece(at, name)
                if name == "xT01":
                    ins = copy(xT[:, 0:2, :], src[0:KC, :].rearrange("p (c n) -> p c n", c=2))
                elif name == "xT2":
                    ins = copy(xT[:, 2, :], src[0:KC, 0:2 * S])
                elif name == "ctxT":
                    ins = copy(ctxT[:, :, :], src[0:CC, :].rearrange("p (c n) -> p c n", c=2))
                elif name == "MT":
                    ins = copy(m[:, :].rearrange("k (b n) -> k b n", b=2),
                               src[:, 0:2 * KL].rearrange("k (b n) -> k b n", b=2)[:, :, HID - QC:KL])
                elif name == "XG":
                    ins = copy(xg[:, :, :, 0:HT],
                               src.rearrange("k (b h n) -> k b h n", b=2, h=HEADS))
                elif name == "QT01":
                    ins = copy(qT[:, par, 0:2, :], src[0:KC, :].rearrange("p (c n) -> p c n", c=2),
                               SCALE)
                elif name == "QM":
                    ins = copy(qT[0:KL, par, 2, :], src[0:KL, 0:2 * S], SCALE)
                else:
                    ins = copy(v_sb[0:KEYS, par, int(name[1]), :], src[0:KEYS, 0:HID])
                ins.then_inc(a_drained, 1)

            def turn_out(at, name, dst):
                src = piece(at, name)
                copy(dst, src[0:KC, 0:NC * S].rearrange("p (c n) -> p c n", c=NC)) \
                    .then_inc(a_drained, 1)

            def exps_turned(n):
                for half in range(2):
                    act.wait_ge(turned_full, n * 2 + (half + 1))
                    nc.scalar.activation(probsT[:, 4 * half:4 * half + 4, :],
                                         turned[half].rearrange("k (h q) -> k h q", h=4), ACT.Exp) \
                        .then_inc(exped, 1)

            def exps(n, par, keys):
                for half in range(2):
                    act.wait_ge(maxed, n * 2 + (half + 1))
                    for h in range(4 * half, 4 * half + 4):
                        k = h % 4
                        last = nc.scalar.activation(
                            probs[:, h, 0:keys], scores[half][:, k * keys:(k + 1) * keys], ACT.Exp,
                            bias=neg_max[:, h:h + 1], accum_out=sums[:, par, h:h + 1])
                    last.then_inc(exped, 1)

            for name in ("WcaT", "caQ", "caT", "WqT0", "WqT1"):
                setup(name)
            front("prologue", "QM")
            setup("WqT2")
            front("prologue", "MT")
            src = piece("prologue", "ctxT")[0:CC, :].rearrange("p (c n) -> p c n", c=2)
            copy(ctxT_r[0][:], src).then_inc(ctx_split, 1)
            copy(ctxT[:], src).then_inc(a_drained, 1)
            setup("k2T")
            front("prologue", "QT01")
            setup("G0")
            front("prologue", "V0")
            setup("G2")
            front("prologue", "V1")
            front("prologue", "XG")

            def exps3(at):
                act.wait_ge(less3_made, at.lin(1, 1))
                nc.scalar.activation(exp3[:], less3[:], ACT.Exp, scale=SCALE).then_inc(exp3_made, 1)

            def copy_probs3(at):
                src = piece(at, "P3T")
                copy(probs3T[:, :, :], src[:, 0:2 * S].rearrange("p (b n) -> p b n", b=2)) \
                    .then_inc(a_drained, 1)

            def body(at):
                more, first = at.kind != "last", at.kind == "first"
                if not first:
                    copy_probs3(at)
                if more and not first:
                    front(at, "ctxT")
                exps_turned(unit(at, 0))
                if first:
                    front(at, "ctxT")
                if not first:
                    turn_out(at, "hsT0", hsT[:, 0])
                    turn_out(at, "hsT1", hsT[:, 1])
                if more:
                    front(at, "xT01")
                    front(at, "xT2")
                exps_turned(unit(at, 1))
                exps(unit(at, 2), 0, KEYS)
                if more:
                    front(at, "QM")
                    front(at, "MT")
                    front(at, "XG")
                    exps3(at)
                exps(unit(at, 3), 1, KEYS)
                if not more:
                    exps3(at)
                if more:
                    front(at, "QT01")
                    front(at, "V0")
                    front(at, "V1")

            pairs(act, body)
            turn_out("epilogue", "hsT0", hsT[:, 0])
            turn_out("epilogue", "hsT1", hsT[:, 1])
            copy_probs3("epilogue")

        @block.vector
        def _(dve):
            v = nc.vector

            def copy(dst, src):
                return v.tensor_copy(dst, src)

            def piece(at, name):
                n, bank = RING_D.no(at, name)
                dve.wait_ge(d_filled, n + 1)
                return bank_d[bank]

            v.memset(ca_now[:].bitcast(U32), 0)
            v.memset(ca_less[:].bitcast(U32), 0)
            v.memset(ca_stack[:, :, :, T * len(CA_PART):], 0.0).then_inc(ca_split, 1)
            dve.wait_ge(loaded_ca, 16)
            v.tensor_copy(ca_sel[:, :].rearrange("r (n two) -> r n two", two=2),
                          ca_all[:, :].rearrange("r (n three) -> r n three", three=3)[:, :, 0:2]) \
                .then_inc(ca_picked, 1)
            dve.wait_ge(ca_picked, 1)
            v.tensor_copy(ca_sel[:, S - 1:S], ca_all[:, CAD - 1:CAD]).then_inc(ca_picked, 1)
            dve.wait_ge(loaded_wq, 32)
            copy(wq_r[0][:, :, 0:HID], wq[:, :, 0:HID]).then_inc(wq_split, 1)
            dve.wait_ge(wq_split, 1)
            v.tensor_tensor(wq_r[1][:, :, 0:HID], wq[:, :, 0:HID], wq_r[0][:, :, 0:HID],
                            ALU.subtract).then_inc(wq_split, 1)

            def stack_ca():
                def steps_done(n):
                    dve.wait_ge(ca_split, n)
                v.tensor_copy(ca_parts[:, 0, :], caQ[:, :]).then_inc(ca_split, 1)
                steps_done(2)
                v.tensor_tensor(ca_rest[:, :], caQ[:, :], ca_parts[:, 0, :], ALU.subtract) \
                    .then_inc(ca_split, 1)
                steps_done(3)
                v.tensor_copy(ca_parts[:, 1, :], ca_rest[:, :]).then_inc(ca_split, 1)
                steps_done(4)
                for slot, part in enumerate(CA_PART):
                    dst = ca_stack[:, :, :, T * slot:T * slot + T]
                    wide = [t.rearrange("q (b t) -> q b t", t=T).unsqueeze(2)
                            .broadcast_to([S, B, 4, T])
                            for t in (ca_parts[:, 0, :], ca_parts[:, 1, :], ca_rest[:, :])]
                    if part == 2:
                        v.tensor_tensor(dst, wide[2], wide[1], ALU.subtract).then_inc(ca_split, 1)
                    else:
                        v.tensor_copy(dst, wide[part]).then_inc(ca_split, 1)

            def ca_rows_out(src, n):
                return copy(ca_rows[:, 8 * n:8 * n + 8, :],
                            src.bitcast(BF16).rearrange("p (b q) -> p b q", b=8))

            def pick_ca(row):
                for j in range(4):
                    rows = slice(32 * j, 32 * j + 32)
                    copy(ca_now[rows, :, j, :], ca_rows[rows, bass.ds(row, 2), :])

            def late(at, step):
                for name in LATE_D[step]:
                    src = piece(at, name)
                    if name == "v2T":
                        for c in range(NC):
                            ins = v.tensor_tensor(
                                v2_blocks[:, c].rearrange("p b (h t) -> p b h t", h=HEADS),
                                src[0:KC, c * B * T:(c + 1) * B * T]
                                    .rearrange("p (b t) -> p b t", b=B)
                                    .unsqueeze(2).broadcast_to([KC, B, HEADS, T]),
                                hmask[:, c].unsqueeze(1).broadcast_to([KC, B, HEADS, T]), ALU.mult)
                    elif name == "CA1":
                        ins = ca_rows_out(src, 1)
                    else:
                        n = int(name[2])
                        copy(vw_parts[0][:, n, :], src[:, 0:HID]).then_inc(vw_high, 1)
                        dve.wait_ge(vw_high, n + 1)
                        ins = v.tensor_tensor(vw_parts[1][:, n, :], src[:, 0:HID],
                                              vw_parts[0][:, n, :], ALU.subtract)
                    ins.then_inc(d_drained, 1)

            def front(at, name):
                par = 0 if at == "prologue" else 1 - at.par
                src = piece(at, name)
                if name == "KT01":
                    for j in range(3):
                        for c in range(2):
                            ins = v.tensor_scalar(
                                k_blocks[:, c, j],
                                src[0:KC, c * 2 * KEYS:(c + 1) * 2 * KEYS]
                                    .rearrange("p (b k) -> p b k", b=2),
                                hmask[:, 0, j, 0:1], None, ALU.mult)
                elif name == "KT2":
                    for j in range(2):
                        ins = v.tensor_scalar(
                            k_last[:, par, j],
                            src[0:KL, 0:2 * KEYS].rearrange("p (b k) -> p b k", b=2),
                            hmask[0:KL, 0, j, 0:1], None, ALU.mult)
                else:
                    ins = copy(m_rows[:, :, :, :],
                               src[:, 0:2 * S].bitcast(BF16)
                                   .rearrange("p (b g n) -> p b g n", b=2, g=2))
                ins.then_inc(d_drained, 1)

            def maxima(n, keys):
                for half in range(2):
                    dve.wait_ge(scored, n * 2 + (half + 1))
                    v.tensor_reduce(neg_max[:, 4 * half:4 * half + 4],
                                    scores[half][:, 0:4 * keys].rearrange("q (h k) -> q h k", h=4),
                                    AX.X, ALU.max, negate=True).then_inc(maxed, 1)

            def split_max(at, b):
                done, base = at.lin(8, 4 * b), at.lin(2, b)
                part = ca_stack[:, bass.ds(base, 1), :, MAX_COL:MAX_COL + 6] \
                    .rearrange("q o j (f t) -> q o f j t", f=2)
                whole, rest = [t.rearrange("q (o f j) -> q o f j", o=1, f=2)
                               for t in (neg_max[:], max_rest[:])]
                dve.wait_ge(maxed, at.lin(8, 2 * b + 2))
                copy(part[:, :, :, :, 0], whole).then_inc(max_split, 1)
                dve.wait_ge(max_split, done + 1)
                v.tensor_tensor(rest, whole, part[:, :, :, :, 0], ALU.subtract) \
                    .then_inc(max_split, 1)
                dve.wait_ge(max_split, done + 2)
                copy(part[:, :, :, :, 1], rest).then_inc(max_split, 1)
                dve.wait_ge(max_split, done + 3)
                v.tensor_tensor(part[:, :, :, :, 2], rest, part[:, :, :, :, 1], ALU.subtract) \
                    .then_inc(max_split, 1)

            def place(at, b):
                dve.wait_ge(stack_turned, at.lin(2, b + 1))
                src = scores[0].bitcast(BF16)
                for j in range(4):
                    rows = slice(32 * j, 32 * j + 32)
                    last = copy(ca_less[rows, j, :], src[rows, 0:S])
                last.then_inc(placed, 1)

            def turned_copy(n, keys):
                for half in range(2):
                    dve.wait_ge(turned_full, n * 2 + (half + 1))
                    copy(probsT[0:keys, 4 * half:4 * half + 4, :],
                         turned[half][0:keys, :].rearrange("k (h q) -> k h q", h=4)) \
                        .then_inc(turned_out, 1)

            def norm(at, k):
                n = unit(at, k)
                if k < 2:
                    src = piece(at, f"PV{k}")[:, 0:HEADS * (HT + 1)] \
                        .rearrange("q (h n) -> q h n", h=HEADS)
                    v.reciprocal(recip[:, k, :], src[:, :, HT]).then_inc(inverted, 1)
                    dve.wait_ge(inverted, n + 1)
                    v.tensor_tensor(by_head[:, k], src[:, :, 0:HT],
                                    recip[:, k, :].unsqueeze(2).broadcast_to([S, HEADS, HT]),
                                    ALU.mult).then_inc(d_drained, 1)
                    dve.wait_ge(d_drained, RING_D.no(at, f"PV{k}")[0] + 1)
                    v.tensor_reduce(scores3[:, k, :], by_head[:, k].rearrange("q h n -> q n h"),
                                    AX.X, ALU.add).then_inc(scores3_made, 1)
                    return
                dve.wait_ge(exped, n * 2 + 2)
                v.reciprocal(recip[:, k % 2, :], sums[:, k % 2, :]).then_inc(inverted, 1)
                src = piece(at, f"PV{k}")
                dve.wait_ge(inverted, n + 1)
                v.tensor_tensor(hs[:, k - 2, 0:HID].rearrange("q (h d) -> q h d", h=HEADS),
                                src[:, 0:HID].rearrange("q (h d) -> q h d", h=HEADS),
                                recip[:, k % 2, :].unsqueeze(2).broadcast_to([S, HEADS, D]),
                                ALU.mult).then_inc(d_drained, 1)

            def softmax3_start(at):
                src = scores3[:].rearrange("q b (h t) -> q (b h) t", t=T)
                dve.wait_ge(scores3_made, at.lin(2, 2))
                v.tensor_reduce(max3[:], src, AX.X, ALU.max).then_inc(max3_made, 1)
                dve.wait_ge(max3_made, at.lin(1, 1))
                v.tensor_tensor(less3[:], src,
                                max3[:].unsqueeze(2).broadcast_to([S, 2 * HEADS, T]),
                                ALU.subtract).then_inc(less3_made, 1)

            def softmax3_end(at):
                dve.wait_ge(exp3_made, at.lin(1, 1))
                v.tensor_reduce(sum3[:, 0, :], exp3[:], AX.X, ALU.add).then_inc(sum3_made, 1)
                dve.wait_ge(sum3_made, at.lin(1, 1))
                v.reciprocal(sum3[:, 1, :], sum3[:, 0, :]).then_inc(inv3_made, 1)
                dve.wait_ge(inv3_made, at.lin(1, 1))
                v.tensor_tensor(p3[:].rearrange("q b (h t) -> q (b h) t", t=T), exp3[:],
                                sum3[:, 1, :].unsqueeze(2).broadcast_to([S, 2 * HEADS, T]),
                                ALU.mult).then_inc(probs3_made, 1)
                dve.wait_ge(probs3_made, at.lin(3, 1))
                wide = p3[:].unsqueeze(2).broadcast_to([S, 2, 2, HT])
                copy(probs3[:, :, 0:2, :], wide).then_inc(probs3_made, 1)
                dve.wait_ge(probs3_made, at.lin(3, 2))
                v.tensor_tensor(probs3[:, :, 2:4, :], wide, probs3[:, :, 0:2, :],
                                ALU.subtract).then_inc(probs3_made, 1)

            def split_hidden(at, b):
                base = 4 * (PAIRS - 1) if at == "epilogue" else at.lin(4, -4)
                dve.wait_ge(a_drained, RING_A.no(at, f"hsT{b}")[0] + 1)
                copy(hsT_r[0][:, b], hsT[:, b]).then_inc(hs_split, 1)
                dve.wait_ge(hs_split, base + (2 * b + 1))
                v.tensor_tensor(hsT_r[1][:, b], hsT[:, b], hsT_r[0][:, b], ALU.subtract) \
                    .then_inc(hs_split, 1)

            def finish(at, b, par):
                src = piece(at, f"out{b}")
                if at == "epilogue":
                    dve.wait_ge(xb_made, B)
                    dve.wait_ge(out_free[b], 16 * PAIRS)
                else:
                    dve.wait_ge(xb_made, at.lin(2))
                    dve.wait_ge(out_free[b], at.lin(16))
                v.tensor_tensor(out_sb[:, b, :], src[:, 0:HID], xb[:, par, b, :], ALU.add) \
                    .then_inc(d_drained, 1)

            def low_ctx():
                dve.wait_ge(a_drained, RING_A.no("prologue", "ctxT")[0] + 1)
                v.tensor_tensor(ctxT_r[1][:], ctxT[:], ctxT_r[0][:], ALU.subtract) \
                    .then_inc(ctx_split, 1)

            def low_x(name, chunks):
                dve.wait_ge(a_drained, RING_A.no("prologue", name)[0] + 1)
                v.tensor_tensor(xT_r[1][:, chunks], xT[:, chunks], xT_r[0][:, chunks],
                                ALU.subtract).then_inc(x_split, 1)

            def place_wca():
                own = slice(HID, QW)
                dve.wait_ge(made, 5)
                dve.wait_ge(a_drained, RING_A.no("prologue", "WcaT")[0] + 1)
                v.tensor_tensor(wq[:, :, own].rearrange("p c (h t) -> p c h t", h=HEADS),
                                wca_t[:].unsqueeze(2).broadcast_to([KC, NC, HEADS, T]),
                                hmask[:], ALU.mult).then_inc(wca_step, 1)
                dve.wait_ge(wca_step, 1)
                copy(wq_r[0][:, :, own], wq[:, :, own]).then_inc(wca_step, 1)
                dve.wait_ge(wca_step, 2)
                v.tensor_tensor(wq_r[1][:, :, own], wq[:, :, own], wq_r[0][:, :, own],
                                ALU.subtract).then_inc(wca_step, 1)

            def stack_m():
                dve.wait_ge(a_drained, RING_A.no("prologue", "MT")[0] + 1)
                copy(m_parts[:, 0, :], m[:, :]).then_inc(m_step, 1)
                dve.wait_ge(m_step, 1)
                v.tensor_tensor(m_rest[:, :], m[:, :], m_parts[:, 0, :], ALU.subtract) \
                    .then_inc(m_step, 1)
                dve.wait_ge(m_step, 2)
                copy(m_parts[:, 1, :], m_rest[:, :]).then_inc(m_step, 1)
                dve.wait_ge(m_step, 3)
                wide = [t.rearrange("k (bh t) -> k bh t", t=T)
                        for t in (m_parts[:, 0, :], m_parts[:, 1, :], m_rest[:, :])]
                for slot, part in enumerate(M_PART):
                    dst = m_stack[:, :, :, T * slot:T * slot + T].rearrange("k b h t -> k (b h) t")
                    if part == 2:
                        v.tensor_tensor(dst, wide[2], wide[1], ALU.subtract).then_inc(m_step, 1)
                    else:
                        copy(dst, wide[part]).then_inc(m_step, 1)

            low_x("xT01", slice(0, 2))
            low_x("xT2", slice(2, 3))
            place_wca()
            dve.wait_ge(a_drained, RING_A.no("prologue", "caQ")[0] + 1)
            stack_ca()
            ca_rows_out(piece("prologue", "CA0"), 0).then_inc(d_drained, 1)
            dve.wait_ge(d_drained, RING_D.no("prologue", "CA0")[0] + 1)
            pick_ca(0)
            stack_m()
            low_ctx()
            front("prologue", "MsT")
            maxima(0, S)
            split_max(At(0, 0, 0, "first"), 0)
            g_out(lambda o, i, mask: v.tensor_scalar(o, i, mask, None, ALU.mult),
                  piece("prologue", "G1"), 1).then_inc(d_drained, 1)
            front("prologue", "KT2")
            place(At(0, 0, 0, "first"), 0)
            front("prologue", "KT01")

            def body(at):
                more, first = at.kind != "last", at.kind == "first"
                maxima(unit(at, 1), S)
                if not first:
                    split_hidden(at, 0)
                split_max(at, 1)
                if more:
                    norm(at, 0)
                place(at, 1)
                if not more:
                    norm(at, 0)
                if first:
                    late(at, 0)
                else:
                    finish(at, 0, 1 - at.par)
                    split_hidden(at, 1)
                if more:
                    front(at, "KT2")
                maxima(unit(at, 2), KEYS)
                if first:
                    late(at, 1)
                else:
                    finish(at, 1, 1 - at.par)
                if more:
                    norm(at, 1)
                    softmax3_start(at)
                turned_copy(unit(at, 2), KEYS)
                maxima(unit(at, 3), KEYS)
                if not more:
                    norm(at, 1)
                    softmax3_start(at)
                if more:
                    front(at, "KT01")
                if first:
                    late(at, 2)
                if more:
                    softmax3_end(at)
                    pick_ca(at.lin(2, 2))
                    front(at, "MsT")
                norm(at, 2)
                turned_copy(unit(at, 3), KEYS)
                if more:
                    maxima(unit(at, 4), S)
                    split_max(at.next(), 0)
                if first:
                    late(at, 3)
                if more:
                    place(at.next(), 0)
                else:
                    split_hidden("epilogue", 0)
                norm(at, 3)
                if not more:
                    softmax3_end(at)

            pairs(dve, body)
            split_hidden("epilogue", 1)
            finish("epilogue", 0, (PAIRS - 1) % 2)
            finish("epilogue", 1, (PAIRS - 1) % 2)

        @block.tensor
        def _(pe):
            mm = nc.tensor.matmul

            def fill_a(at, name):
                n, bank = RING_A.no(at, name)
                if not (isinstance(n, int) and n < 2):
                    pe.wait_ge(a_drained, n - 1)
                return bank_a[bank]

            def fill_d(at, name):
                n, bank = RING_D.no(at, name)
                if not (isinstance(n, int) and n < 2):
                    pe.wait_ge(d_drained, n - 1)
                return bank_d[bank]

            def got_a(at, name):
                pe.wait_ge(a_drained, RING_A.no(at, name)[0] + 1)

            def got_d(at, name):
                pe.wait_ge(d_drained, RING_D.no(at, name)[0] + 1)

            def turn(dst, src, rows, eye=None):
                return nc.tensor.transpose(dst, src, (ident if eye is None else eye)[0:rows, 0:rows])

            def three(dst, stationary, moving, first=True, last=True):
                for i, (a, b) in enumerate(((0, 0), (0, 1), (1, 0))):
                    ins = mm(dst, stationary(a), moving(b), start=first and i == 0,
                             stop=last and i == 2)
                return ins

            def setup(name):
                dst = (fill_d if name == "G1" else fill_a)("prologue", name)
                if name == "WcaT":
                    pe.wait_ge(loaded_wqca, 16)
                    for c in range(NC):
                        last = turn(dst[0:KC, c * T:(c + 1) * T], wq_ca[:, c * KC:(c + 1) * KC], T)
                elif name == "caQ":
                    pe.wait_ge(ca_picked, 2)
                    last = turn(dst[:, 0:B * T], ca_sel[:, :], B * T)
                elif name == "caT":
                    pe.wait_ge(loaded_ca, 16)
                    for c in range(2):
                        last = turn(dst[0:CC, c * B * T:(c + 1) * B * T],
                                    ca_all[:, c * CC:(c + 1) * CC], B * T)
                elif name[:3] == "WqT":
                    pe.wait_ge(loaded_wq, 32)
                    c = int(name[3])
                    n = KC if c < 2 else HID - 2 * KC
                    for r in range(NC):
                        last = turn(dst[0:n, r * KC:(r + 1) * KC], wq[:, r, c * KC:c * KC + n], KC)
                elif name == "k2T":
                    last = project_ca(dst, wk_ca)
                else:
                    got_a("prologue", "k2T")
                    r = int(name[1])
                    for c in range(NC):
                        rows, heads = (KC, 3) if c < 2 else (HID - 2 * KC, 2)
                        width = B * heads * T
                        last = mm(dst[0:KC, c * B * 3 * T:c * B * 3 * T + width],
                                  wqT[0:rows, c, r * KC:(r + 1) * KC],
                                  k2_blocks[0:rows, c, :, 0:heads * T], start=True, stop=True)
                last.then_inc(d_filled if name == "G1" else a_filled, 1)

            def project_ca(dst, w):
                pe.wait_ge(loaded_wca, 32)
                pe.wait_ge(made, 13)
                got_a("prologue", "caT")
                for c in range(NC):
                    for r in range(2):
                        last = mm(dst[0:KC, c * B * T:(c + 1) * B * T],
                                  w[:, r, c * KC:(c + 1) * KC], caT[:, r, :],
                                  start=r == 0, stop=r == 1)
                return last

            def late(at, step):
                for name in LATE_D[step]:
                    dst = fill_d(at, name)
                    if name == "v2T":
                        last = project_ca(dst, wv_ca)
                    elif name[:2] == "VW":
                        pe.wait_ge(loaded_wout, 32)
                        got_d(at, "v2T")
                        n = int(name[2])
                        for c in range(NC):
                            last = mm(dst[:, 0:HID],
                                      v2_blocks[:, c, 4 * n:4 * n + 4, :].rearrange("p b n -> p (b n)"),
                                      wout[:, c, :], start=c == 0, stop=c == NC - 1)
                    else:
                        last = turn_ca(dst, 1)
                    last.then_inc(d_filled, 1)

            def turn_ca(dst, n):
                for b in range(8):
                    last = turn(dst.bitcast(BF16)[:, b * S:(b + 1) * S],
                                ca_stack[:, 8 * n + b].rearrange("q j n -> q (j n)"), S, ident16)
                return last

            def front(at, name):
                par = 0 if at == "prologue" else 1 - at.par
                seen = 16 if at == "prologue" else at.next().half(16, 16)
                split = (lambda per: per) if at == "prologue" else (lambda per: at.lin(per, 2 * per))
                a = name in RING_A.lists["prologue"]
                dst = (fill_a if a else fill_d)(at, name)
                if name in ("xT01", "xT2"):
                    if name == "xT01":
                        pe.wait_ge(loaded_x[par], seen)
                    for i, c in enumerate((0, 1) if name == "xT01" else (2,)):
                        for b in range(2):
                            last = turn(dst[0:KC, (2 * i + b) * S:(2 * i + b + 1) * S],
                                        x_sb[:, par, b, c * KC:(c + 1) * KC], S)
                elif name == "ctxT":
                    pe.wait_ge(loaded_ctx[par], seen)
                    for c in range(2):
                        for b in range(2):
                            last = turn(dst[0:CC, (2 * c + b) * S:(2 * c + b + 1) * S],
                                        ctx_sb[:, par, b, c * CC:(c + 1) * CC], S)
                elif name in ("QM", "QT01"):
                    if name == "QM":
                        pe.wait_ge(x_split, split(4))
                    for i, c in enumerate((2,) if name == "QM" else (0, 1)):
                        rows = KL if c == 2 else KC
                        for r in range(NC):
                            last = three(dst[0:rows, i * 2 * S:(i + 1) * 2 * S],
                                         lambda k: wq_r[k][:, r, Q_CHUNKS[c]],
                                         lambda k: xT_r[k][:, r, :], r == 0, r == NC - 1)
                elif name == "XG":
                    row = 0 if at == "prologue" else at.lin(2, 2)
                    for b in range(2):
                        for r in range(NC):
                            heads = 3 if r < 2 else 2
                            last = mm(dst[:, (HEADS * b + 3 * r) * HT:(HEADS * b + 3 * r + heads) * HT],
                                      xT[:, r, b * S:(b + 1) * S],
                                      g_blocks[:, r, bass.ds(row + b, 1), 0:heads, :]
                                          .rearrange("p b j n -> p (b j n)"),
                                      start=True, stop=True)
                elif name == "MT":
                    got_a(at, "QM")
                    for b in range(2):
                        last = turn(dst[:, b * KL:(b + 1) * KL],
                                    qT[0:KL, par, 2, b * S:(b + 1) * S], KL)
                elif name in ("KT01", "KT2"):
                    if name == "KT2":
                        pe.wait_ge(ctx_split, split(2))
                    for i, c in enumerate((0, 1) if name == "KT01" else (2,)):
                        rows = KL if c == 2 else KC
                        for r in range(2):
                            last = three(dst[0:rows, i * 2 * KEYS:(i + 1) * 2 * KEYS],
                                         lambda k: wk_r[k][:, r, Q_CHUNKS[c]],
                                         lambda k: ctxT_r[k][:, r, :]
                                         .rearrange("p (b k) -> p b k", b=2)[:, :, 0:KEYS],
                                         r == 0, r == 1)
                elif name in ("V0", "V1"):
                    b = int(name[1])
                    for r in range(2):
                        last = three(dst[0:KEYS, 0:HID],
                                     lambda k: ctxT_r[k][:, r, b * S:b * S + KEYS],
                                     lambda k: wv_r[k][:, r, :], r == 0, r == 1)
                else:
                    pe.wait_ge(m_step, split(9))
                    dst = dst.bitcast(BF16)
                    for b in range(2):
                        for k in range(2):
                            last = turn(dst[:, (2 * b + k) * S:(2 * b + k + 1) * S],
                                        m_stack[:, b, 4 * k:4 * k + 4, :]
                                            .rearrange("q h n -> q (h n)"), S, ident16)
                last.then_inc(a_filled if a else d_filled, 1)

            def channel_scores(n, at, b):
                for half in range(2):
                    for k in range(4):
                        last = mm(scores[half][:, k * S:(k + 1) * S],
                                  ca_now[:, b, k, :], m_rows[:, b, half, :],
                                  start=True, stop=True)
                    last.then_inc(scored, 1)

            def turn_stack(at, b):
                pe.wait_ge(max_split, at.lin(8, 4 * b + 4))
                turn(scores[0].bitcast(BF16)[:, 0:S],
                     ca_stack[:, bass.ds(at.lin(2, b), 1)].rearrange("q o j n -> q (o j n)"),
                     S, ident16).then_inc(stack_turned, 1)

            def scores_turned(at, b):
                pe.wait_ge(placed, at.lin(2, b + 1))
                for half in range(2):
                    mm(turned[half][:, :], m_rows[:, b, half, :],
                       ca_less[:, :, :].rearrange("p j q -> p (j q)"), start=True, stop=True) \
                        .then_inc(turned_full, 1)

            def token_scores(at, b):
                tok = slice(b * S, (b + 1) * S)
                for half, runs in enumerate((((0, 0, 3), (1, 0, 1)), ((1, 1, 2), (2, 0, 2)))):
                    col = 0
                    for c, j, heads in runs:
                        width, rows = heads * KEYS, KL if c == 2 else KC
                        keys = k_last[:, at.par] if c == 2 else k_blocks[:, c]
                        last = mm(scores[half][:, col:col + width], qT[0:rows, at.par, c, tok],
                                  keys[:, j:j + heads, b, :],
                                  start=True, stop=True)
                        col += width
                    last.then_inc(scored, 1)

            def turn_probs(n, keys):
                for half in range(2):
                    pe.wait_ge(exped, n * 2 + (half + 1))
                    for k in range(4):
                        last = turn(turned[half][0:keys, k * S:(k + 1) * S],
                                    probs[:, 4 * half + k, 0:keys], S)
                    last.then_inc(turned_full, 1)

            def weigh(at, k):
                n, b, keys = unit(at, k), k % 2, S if k < 2 else KEYS
                dst = fill_d(at, f"PV{k}")
                for h in range(HEADS):
                    if h % 4 == 0 and k < 2:
                        pe.wait_ge(exped, n * 2 + (h // 4 + 1))
                    elif h % 4 == 0:
                        pe.wait_ge(turned_out, at.lin(4, 2 * b + (h // 4 + 1)))
                    if k < 2:
                        last = mm(dst[:, h * (HT + 1):(h + 1) * (HT + 1)], probsT[:, h, :],
                                  xg[:, b, h, :], start=True, stop=True)
                    else:
                        last = mm(dst[:, h * D:(h + 1) * D], probsT[0:keys, h, :],
                                  v_sb[0:keys, at.par, b, h * D:(h + 1) * D], start=True, stop=True)
                    if k == 3 and h == HEADS - 2 and at.kind != "last":
                        turn_stack(at.next(), 0)
                last.then_inc(d_filled, 1)

            def turn_hidden(at, name, k, after):
                dst = fill_a(at, name)
                pe.wait_ge(d_drained, after + 1)
                for c in range(NC):
                    last = turn(dst[0:KC, c * S:(c + 1) * S], hs[:, k - 2, c * KC:(c + 1) * KC], S)
                last.then_inc(a_filled, 1)

            def turn_probs3(at):
                dst = fill_a(at, "P3T")
                pe.wait_ge(probs3_made, 3 * PAIRS if at == "epilogue" else at.lin(3))
                for b in range(2):
                    last = turn(dst[:, b * S:(b + 1) * S],
                                probs3[:, b].rearrange("q j n -> q (j n)").bitcast(F32), S)
                last.then_inc(a_filled, 1)

            def add_probs3(at, b, dst, **group):
                got_a(at, "P3T")
                pe.wait_ge(vw_stacked, 16 * 16)
                seq = B - 2 + b if at == "epilogue" else at.lin(2, b - 2)
                return mm(dst[:, 0:HID], probs3T[:, b, :],
                          vw_stack[:, bass.ds(seq, 1), :].rearrange("p g n -> p (g n)"), **group)

            def add_hidden(at, b, dst, first, last):
                base = 4 * (PAIRS - 1) if at == "epilogue" else at.lin(4, -4)
                pe.wait_ge(hs_split, base + (2 * b + 2))
                for c in range(NC):
                    ins = three(dst[:, 0:HID], lambda k: hsT_r[k][:, b, c, :],
                                lambda k: wout_r[k][:, c, :], first and c == 0, last and c == NC - 1)
                    if b == c == 0 and at != "epilogue":
                        turn_stack(at, 1)
                return ins

            def project(at, b):
                dst = fill_d(at, f"out{b}")
                add_probs3(at, b, dst, start=True, stop=False)
                add_hidden(at, b, dst, False, True).then_inc(d_filled, 1)

            pe.wait_ge(made, 2)
            pe.wait_ge(zeroed, 3)
            front("prologue", "xT01")
            front("prologue", "xT2")
            for name in ("WcaT", "caQ", "caT", "WqT0", "WqT1"):
                setup(name)
            pe.wait_ge(wca_step, 3)
            front("prologue", "QM")
            setup("WqT2")
            pe.wait_ge(ca_split, 4 + len(CA_PART))
            pe.wait_ge(made, 10)
            dst = fill_d("prologue", "CA0")
            turn_ca(dst, 0).then_inc(d_filled, 1)
            front("prologue", "MT")
            front("prologue", "ctxT")
            setup("k2T")
            front("prologue", "QT01")
            front("prologue", "MsT")
            setup("G0")
            got_d("prologue", "MsT")
            channel_scores(0, At(0, 0, 0, "first"), 0)
            setup("G1")
            pe.wait_ge(w_parts, 4)
            front("prologue", "V0")
            front("prologue", "KT2")
            turn_stack(At(0, 0, 0, "first"), 0)
            setup("G2")
            front("prologue", "V1")
            front("prologue", "KT01")
            got_a("prologue", "G2")
            got_d("prologue", "G1")
            front("prologue", "XG")

            def body(at):
                more, first = at.kind != "last", at.kind == "first"
                if not first:
                    turn_probs3(at)
                if more and not first:
                    front(at, "ctxT")
                scores_turned(at, 0)
                channel_scores(unit(at, 1), at, 1)
                if first:
                    front(at, "ctxT")
                if not first:
                    prev = RING_D.no(at, "PV0")[0] - 1
                    turn_hidden(at, "hsT0", 2, prev)
                    turn_hidden(at, "hsT1", 3, prev)
                pe.wait_ge(made, 15)
                weigh(at, 0)
                if more:
                    front(at, "xT01")
                    front(at, "xT2")
                if first:
                    late(at, 0)
                    turn_stack(at, 1)
                else:
                    project(at, 0)
                if more:
                    front(at, "KT2")
                scores_turned(at, 1)
                token_scores(at, 0)
                if first:
                    late(at, 1)
                    pe.wait_ge(w_parts, 6)
                else:
                    project(at, 1)
                weigh(at, 1)
                if more:
                    front(at, "QM")
                turn_probs(unit(at, 2), KEYS)
                token_scores(at, 1)
                if more:
                    front(at, "MT")
                    front(at, "KT01")
                    front(at, "XG")
                if first:
                    late(at, 2)
                if more:
                    front(at, "QT01")
                    front(at, "MsT")
                weigh(at, 2)
                turn_probs(unit(at, 3), KEYS)
                if more:
                    got_d(at, "MsT")
                    channel_scores(unit(at, 4), at.next(), 0)
                    if first:
                        late(at, 3)
                    front(at, "V0")
                    front(at, "V1")
                else:
                    turn_hidden("epilogue", "hsT0", 2, RING_D.no(at, "PV2")[0])
                weigh(at, 3)

            pairs(pe, body)
            dst = fill_d("epilogue", "out0")
            add_hidden("epilogue", 0, dst, True, False)
            turn_hidden("epilogue", "hsT1", 3, RING_D.no("epilogue", "out0")[0] - 1)
            turn_probs3("epilogue")
            add_probs3("epilogue", 0, dst, start=False, stop=True).then_inc(d_filled, 1)
            dst = fill_d("epilogue", "out1")
            add_probs3("epilogue", 1, dst, start=True, stop=False)
            add_hidden("epilogue", 1, dst, False, True).then_inc(d_filled, 1)


_INS = ['x', 'ctx_768', 'L0_xattn_Wq', 'L0_xattn_Wk', 'L0_xattn_Wv', 'L0_xattn_Wq_ca', 'L0_xattn_Wk_ca',
        'L0_xattn_Wv_ca', 'L0_xattn_Wout', 'L0_xattn_b_out']


def kernel(**inputs):
    import numpy as np
    import concourse.bacc as bacc
    from concourse import mybir as mb
    from concourse.bass_utils import run_bass_kernel_spmd

    nc = bacc.Bacc("TRN2", target_bir_lowering=False, num_devices=1)
    arrays, args = {}, []
    for name in _INS:
        a = np.ascontiguousarray(inputs[name])
        arrays[f"in_{name}"] = a
        args.append(nc.dram_tensor(f"in_{name}", a.shape, mb.dt.from_np(a.dtype), kind="ExternalInput").ap())
    args.append(nc.dram_tensor("out_0", (B, S, HID), mb.dt.float32, kind="ExternalOutput").ap())
    attention(nc, *args)
    r = run_bass_kernel_spmd(nc, [arrays], core_ids=[0])
    return r.results[0]["out_0"]
```
